# Optimizing a Trainium2 kernel written in Bass

```python
import numpy as np
import jax
import jax.numpy as jnp

def _softmax(x, axis=-1):
    return jax.nn.softmax(x, axis=axis)

def _gelu(x):
    return jax.nn.gelu(x, approximate=True)

def _silu(x):
    return jax.nn.silu(x)

def _sigmoid(x):
    return jax.nn.sigmoid(x)

def _layernorm(x, axis=-1, eps=1e-05):
    m = jnp.mean(x, axis=axis, keepdims=True)
    v = jnp.var(x, axis=axis, keepdims=True)
    return (x - m) / jnp.sqrt(v + eps)

def _scatter_add(tgt, idx, src, axis=0):
    return tgt.at[idx].add(src)

def _segment_sum(src, seg, n):
    return jax.ops.segment_sum(src, seg, n)
kernel_name = 'mk_adj_resnorm_d1_adj_r2_81a51c'

def setup_inputs(seed: int=0):
    np.random.seed(seed)
    _w = jnp.asarray

    def _rec_inputs():
        import jax
        import jax.numpy as jnp
        _gk = jax.random.key(seed)
        x = -0.006082 + 1.001 * jax.random.normal(jax.random.fold_in(_gk, 1), (4096, 64), jnp.float32)
        _w = (1.0 + jnp.arange(4096, dtype=jnp.float32)) ** (-0.5)
        _w = _w / _w.mean()
        _pij = jnp.clip(0.00195312 * _w[:, None] * _w[None, :], 0.0, 1.0)
        _a = jax.random.uniform(jax.random.fold_in(_gk, 2), (4096, 4096)) < _pij
        adj = _a.astype(jnp.int32)
        return (x, adj)
    x, adj = _rec_inputs()

    def _L0_gnn_setup():
        import jax, jax.numpy as jnp
        import numpy as np
        ALPHA = 0.2
        NEG_INF = -9000000000000000.0
        key = jax.random.key(seed)
        k1, k2, k3, k4 = jax.random.split(key, 4)
        N, F_IN, F_OUT = (512, 64, 64)
        h = jax.random.normal(k1, (N, F_IN), dtype=jnp.float32)
        adj = jax.random.randint(k2, (N, N), 0, 2, dtype=jnp.int32)
        lim_W = 1.414 * np.sqrt(6.0 / (F_IN + F_OUT))
        W = jax.random.uniform(k3, (F_IN, F_OUT), minval=-lim_W, maxval=lim_W, dtype=jnp.float32)
        lim_a = 1.414 * np.sqrt(6.0 / (2 * F_OUT + 1))
        a = jax.random.uniform(k4, (2 * F_OUT, 1), minval=-lim_a, maxval=lim_a, dtype=jnp.float32)
        return {'h': h, 'adj': adj, 'W': W, 'a': a}
    _L0_gnn_all = _L0_gnn_setup()
    _L0_gnn_in = {k: v for k, v in _L0_gnn_all.items() if k in ('W', 'a')}
    del _L0_gnn_all
    return {'x': x, 'adj': adj, 'L0_gnn_W': _L0_gnn_in['W'], 'L0_gnn_a': _L0_gnn_in['a']}

def reference(x, adj, L0_gnn_W, L0_gnn_a):
    import jax
    import jax.numpy as jnp

    def _L0_gnn_ref(h, adj, W, a):
        import jax, jax.numpy as jnp
        import numpy as np
        ALPHA = 0.2
        NEG_INF = -9000000000000000.0
        F_OUT = W.shape[1]
        Wh = h @ W
        a1, a2 = (a[:F_OUT, 0], a[F_OUT:, 0])
        e = (Wh @ a1)[:, None] + (Wh @ a2)[None, :]
        e = jax.nn.leaky_relu(e, negative_slope=ALPHA)
        scores = jnp.where(adj > 0, e, jnp.float32(NEG_INF))
        attention = jax.nn.softmax(scores, axis=1)
        h_prime = attention @ Wh
        return jax.nn.elu(h_prime)
    x = _layernorm(x + _L0_gnn_ref(x, adj, L0_gnn_W, L0_gnn_a), axis=-1)
    return x

_drawn_inputs = setup_inputs


def setup_inputs(seed=0):
    import zlib

    import numpy as np

    out = dict(_drawn_inputs(seed))
    spreads = {}
    factors = {}
    for name, (base, spread) in spreads.items():
        noise = np.random.default_rng([zlib.crc32(name.encode()), seed]).standard_normal(out[name].shape)
        drawn = base * np.exp(spread * noise) if base else spread * noise
        out[name] = jnp.asarray(drawn.astype(out[name].dtype))
    for name, factor in factors.items():
        out[name] = (out[name] * factor).astype(out[name].dtype)
    return out
```

```python
import concourse.bass as bass
from concourse import mybir
from contextlib import ExitStack

F32 = mybir.dt.float32
BF16 = mybir.dt.bfloat16
I32 = mybir.dt.int32
ALU = mybir.AluOpType
ACT = mybir.ActivationFunctionType
AX_X = mybir.AxisListType.X

P = 128
SLOPE = 0.2
EPS = 1e-5

CHUNK = 512
CHUNKS = 2
TURNS = CHUNK // P
TILES = CHUNKS * TURNS
BLOCK = TILES * P
COLS = 32
PAIR = 2
RING = 8
MASKS = 2
PROBS = 8
DVE_STEPS = 12
ACT_STEPS = 3
POOL_STEPS = 6
ACC, DEN = (0, 2), (1, 3)
TURN, TURN_DEN = 4, 5
WH = 2
RAISE = 2.0 ** 60
SUM_WH = 6
BANKS = 8


def gat_layer(nc, xt, xn, w, wt, a, adj, out):
    D = w.shape[0]
    N = 2 * xt.shape[1]
    BLOCKS, PAIRS = adj.shape[0], adj.shape[1]
    JT = N // P
    C = D + 1
    V = D + COLS
    PER_BANK = CHUNK // C
    HALF_BANKS = -(-JT // 2 // PER_BANK)
    FC = N // CHUNK
    FB = BANKS - WH
    assert 2 * D == P and 2 * COLS == D and JT == PAIR * PAIRS and BLOCKS * TILES == JT
    assert PAIRS % RING == 0 and PAIRS % MASKS == 0 and JT % PROBS == 0 and WH + 2 * HALF_BANKS <= BANKS

    with ExitStack() as ctx:
        def sb(name, shape, dt=F32):
            return ctx.enter_context(nc.sbuf_tensor(name, shape, dt))

        def sem(name):
            return ctx.enter_context(nc.semaphore(name))

        xt_s = sb("xt_s", [P, N // 2])
        xn_s = sb("xn_s", [P, BLOCKS, TILES * D])
        wt_s = sb("wt_s", [D, P])
        a_s = sb("a_s", [D, 2])
        w_g = sb("w_g", [P, C])
        wa1 = sb("wa1", [P, P])
        x_sum = sb("x_sum", [P, 1])
        x_copy = sb("x_copy", [P, N // 2], BF16)
        x_sums = sb("x_sums", [P, P])
        ones = sb("ones", [P, P])
        ident = sb("ident", [P, P])
        pick = sb("pick", [P, CHUNKS])
        whg = sb("whg", [P, JT, C])
        g_edge = sb("g_edge", [P, 1])
        g_top = sb("g_top", [1, 1])
        g_max = sb("g_max", [P, 1])
        bias_q = sb("bias_q", [P, 1])
        bias_f = sb("bias_f", [P, 1])
        q = sb("q", [P, JT])
        scale_f = sb("scale_f", [P, JT])
        raised_f = sb("raised_f", [P, JT])
        v = sb("v", [P, JT, V])
        r = sb("r", [P, BLOCKS, BLOCK])
        sum_wh = sb("sum_wh", [P, D])
        ring = sb("ring", [P, RING, PAIR * BLOCK], I32)
        mask = sb("mask", [P, MASKS, PAIR * BLOCK], BF16)
        probs = sb("probs", [P, PROBS, BLOCK])
        acc_s = sb("acc_s", [P, CHUNK])
        den_s = sb("den_s", [P, CHUNK])
        iso = sb("iso", [P, TILES])
        den = sb("den", [P, TILES])
        rden = sb("rden", [P, TILES])
        iso_n = sb("iso_n", [P, TILES])
        h_iso = sb("h_iso", [P, TILES, D])
        h = sb("h", [P, TILES, D])
        h_neg = sb("h_neg", [P, TILES * D])
        h_exp = sb("h_exp", [P, TILES * D])
        res = sb("res", [P, TILES, D])
        row_sum = sb("row_sum", [P, TILES])
        mean = sb("mean", [P, TILES])
        cent = sb("cent", [P, TILES, D])
        sq = sb("sq", [P, TILES, D])
        sq_sum = sb("sq_sum", [P, TILES])
        var = sb("var", [P, TILES])
        minus_half = sb("minus_half", [P, TILES])
        rstd = sb("rstd", [P, TILES])
        y = sb("y", [P, TILES, D])

        ps = ctx.enter_context(nc.psum_tensor("ps", [P, BANKS, CHUNK], F32))
        turned = ps[:, TURN, :].rearrange("p (t d) -> p t d", t=TILES)
        turned_den = ps[:, TURN_DEN, 0:TILES]

        w_landed = sem("w_landed")
        xt_landed = sem("xt_landed")
        xn_landed = sem("xn_landed")
        adj_landed = [sem(f"adj_landed{s}") for s in range(RING)]
        consts_ready = sem("consts_ready")
        pick_steps = sem("pick_steps")
        ident_ready = sem("ident_ready")
        wa_ready = sem("wa_ready")
        w_g_ready = sem("w_g_ready")
        wh_ready = sem("wh_ready")
        whg_ready = sem("whg_ready")
        edge_ready = sem("edge_ready")
        edge_turned = sem("edge_turned")
        top_ready = sem("top_ready")
        top_spread = sem("top_spread")
        g_max_ready = sem("g_max_ready")
        biases_ready = sem("biases_ready")
        factors_ready = sem("factors_ready")
        raised_ready = sem("raised_ready")
        v_ready = sem("v_ready")
        v_den_ready = sem("v_den_ready")
        f_ready = sem("f_ready")
        r_arg_ready = sem("r_arg_ready")
        r_ready = sem("r_ready")
        x_sum_ready = sem("x_sum_ready")
        x_sums_ready = sem("x_sums_ready")
        sum_wh_summed = sem("sum_wh_summed")
        sum_wh_ready = sem("sum_wh_ready")
        mask_ready = sem("mask_ready")
        probs_ready = sem("probs_ready")
        probs_used = sem("probs_used")
        acc_turned = sem("acc_turned")
        act_epi = sem("act_epi")
        dve_epi = sem("dve_epi")
        pool_epi = sem("pool_epi")
        y_stored = sem("y_stored")

        ISO, NUM_ISO, RDEN, H, H_ALL, H_NEG, X_EXP, RES, ROW_SUM, MEAN, SQ_SUM, VAR = range(1, DVE_STEPS + 1)
        TAKE_ACC, TAKE_DEN, ELU_EXP = range(1, ACT_STEPS + 1)
        ISO_N, H_ISO, CENT, SQ, RSTD, Y = range(1, POOL_STEPS + 1)

        def over_cols(per_tile):
            return per_tile.unsqueeze(2).to_broadcast([P, per_tile.shape[1], D])

        def over_tiles(row):
            return row.unsqueeze(1).to_broadcast([P, TILES, D])

        def wh_place(jt):
            half, at = jt // (JT // 2), jt % (JT // 2)
            return WH + half * HALF_BANKS + at // PER_BANK, at % PER_BANK * C

        block = ctx.enter_context(nc.Block())

        @block.sync
        def _(sp):
            sp.dma_start(wt_s[:, 0:D], wt).then_inc(w_landed, 16)
            sp.dma_start(wt_s[:, D:P], wt).then_inc(w_landed, 16)
            sp.dma_start(a_s[:, :], a).then_inc(w_landed, 16)
            sp.dma_start(xt_s[:, :], xt).then_inc(xt_landed, 16)

            def load(b, k, filled):
                if filled:
                    sp.wait_ge(mask_ready, b * PAIRS + k - RING + 1)
                sp.dma_start(ring[:, k % RING, :], adj[b, k]).then_inc(adj_landed[k % RING], 16)

            for k in range(RING):
                load(0, k, False)
            sp.dma_start(xn_s[:, :, :], xn).then_inc(xn_landed, 16)
            for k in range(RING, PAIRS):
                load(0, k, True)
            with sp.Fori(1, BLOCKS) as b:
                for k in range(PAIRS):
                    load(b, k, True)

        @block.gpsimd
        def _(pool):
            pool.memset(ones[:, :], 1.0).then_inc(consts_ready, 1)
            pool.memset(minus_half[:, :], -0.5).then_inc(consts_ready, 1)
            pool.wait_ge(consts_ready, 2)
            pool.affine_select(out=ident[:, :], in_=ones[:, :], compare_op=ALU.is_equal, fill=0.0, base=0,
                               pattern=[[-1, P]], channel_multiplier=1).then_inc(ident_ready, 1)
            pool.affine_select(out=pick[:, :], in_=ones[:, 0:CHUNKS], compare_op=ALU.is_equal, fill=0.0, base=0,
                               pattern=[[-COLS, CHUNKS]], channel_multiplier=1).then_inc(pick_steps, 1)
            pool.wait_ge(pick_steps, 1)
            pool.affine_select(out=pick[:, :], in_=pick[:, :], compare_op=ALU.not_equal, fill=1.0,
                               base=-CHUNKS * COLS, pattern=[[-COLS, CHUNKS]],
                               channel_multiplier=1).then_inc(pick_steps, 1)
            pool.wait_ge(raised_ready, 1)
            pool.tensor_copy(v[:, :, D:V], raised_f[:, :].unsqueeze(2).to_broadcast([P, JT, COLS]))\
                .then_inc(v_den_ready, 1)
            pool.wait_ge(sum_wh_ready, 1)

            with pool.Fori(0, BLOCKS) as b:
                pool.wait_ge(dve_epi, b * DVE_STEPS + RDEN)
                pool.tensor_tensor(iso_n[:, :], iso[:, :], rden[:, :], ALU.mult).then_inc(pool_epi, 1)
                pool.wait_ge(pool_epi, b * POOL_STEPS + ISO_N)
                pool.tensor_tensor(h_iso[:, :, :], over_tiles(sum_wh[:, :]), over_cols(iso_n[:, :]),
                                   ALU.mult).then_inc(pool_epi, 1)
                pool.wait_ge(dve_epi, b * DVE_STEPS + MEAN)
                pool.tensor_tensor(cent[:, :, :], res[:, :, :], over_cols(mean[:, :]), ALU.subtract)\
                    .then_inc(pool_epi, 1)
                pool.wait_ge(pool_epi, b * POOL_STEPS + CENT)
                pool.tensor_tensor(sq[:, :, :], cent[:, :, :], cent[:, :, :], ALU.mult).then_inc(pool_epi, 1)
                pool.wait_ge(dve_epi, b * DVE_STEPS + VAR)
                pool.tensor_tensor(rstd[:, :], var[:, :], minus_half[:, :], ALU.pow).then_inc(pool_epi, 1)
                pool.wait_ge(pool_epi, b * POOL_STEPS + RSTD)
                pool.wait_ge(y_stored, 16 * b)
                pool.tensor_tensor(y[:, :, :], cent[:, :, :], over_cols(rstd[:, :]), ALU.mult)\
                    .then_inc(pool_epi, 1)

        @block.scalar
        def _(act):
            def make_mask(b, k, slot_used):
                act.wait_ge(adj_landed[k % RING], 16 * (b * (PAIRS // RING) + k // RING + 1))
                if slot_used:
                    act.wait_ge(probs_ready, PAIR * (b * PAIRS + k - MASKS + 1))
                act.activation(mask[:, k % MASKS, :], ring[:, k % RING, :], ACT.Relu).then_inc(mask_ready, 1)

            def take_sums(b):
                act.wait_ge(probs_used, (b + 1) * PAIRS)
                act.activation(acc_s[:, :], ps[:, ACC[0] + (ACC[1] - ACC[0]) * (b % 2), :], ACT.Copy)\
                   .then_inc(act_epi, 1)
                act.activation(den_s[:, :], ps[:, DEN[0] + (DEN[1] - DEN[0]) * (b % 2), :], ACT.Copy)\
                   .then_inc(act_epi, 1)

            def elu_exp(b):
                act.wait_ge(dve_epi, b * DVE_STEPS + H_NEG)
                act.activation(h_exp[:, :], h_neg[:, :], ACT.Exp).then_inc(act_epi, 1)

            def store(b):
                act.wait_ge(pool_epi, b * POOL_STEPS + Y)
                act.dma_start(out[:, b, :], y[:, :, :].rearrange("p t d -> p (t d)")).then_inc(y_stored, 16)

            def r_chunk(c):
                act.wait_ge(r_arg_ready, c + 1)
                b, at = c // CHUNKS, c % CHUNKS * CHUNK
                act.activation(r[:, b, at:at + CHUNK], r[:, b, at:at + CHUNK], ACT.Exp, scale=-(1 - SLOPE))\
                   .then_inc(r_ready, 1)

            act.dma_start(w_g[0:D, 0:D], w).then_inc(w_landed, 16)
            act.dma_start(w_g[D:P, 0:D], w).then_inc(w_landed, 16)
            act.wait_ge(xt_landed, 16)
            act.activation(x_copy[:, :], xt_s[:, :], ACT.Copy, accum_out=x_sum[:, :]).then_inc(x_sum_ready, 1)
            act.wait_ge(biases_ready, 2)
            act.activation(scale_f[:, :], whg[:, :, D], ACT.Exp, bias=bias_f[:, :], scale=SLOPE)\
               .then_inc(factors_ready, 1)
            act.activation(q[:, :], whg[:, :, D], ACT.Exp, bias=bias_q[:, :], scale=1 - SLOPE)\
               .then_inc(factors_ready, 1)
            for c in range(CHUNKS):
                r_chunk(c)
            for k in range(PAIRS):
                make_mask(0, k, k >= MASKS)
                if CHUNKS <= k < FC:
                    r_chunk(k)
            with act.Fori(1, BLOCKS) as b:
                for k in range(PAIRS):
                    make_mask(b, k, True)
                    if k == 3:
                        take_sums(b - 1)
                    if k == 9:
                        elu_exp(b - 1)
                store(b - 1)
            take_sums(BLOCKS - 1)
            elu_exp(BLOCKS - 1)
            store(BLOCKS - 1)
            act.wait_ge(y_stored, 16 * BLOCKS)

        @block.vector
        def _(dve):
            def weights(b, jt, slot_used):
                k = jt // PAIR
                if jt % PAIR == 0:
                    dve.wait_ge(mask_ready, b * PAIRS + k + 1)
                    if slot_used:
                        dve.wait_ge(probs_used, b * PAIRS + k - PROBS // PAIR + 1)
                dve.scalar_tensor_tensor(out=probs[:, jt % PROBS, :], in0=r[:, b, :], scalar=q[:, jt:jt + 1],
                                         in1=mask[:, k % MASKS, (jt % PAIR) * BLOCK:(jt % PAIR + 1) * BLOCK],
                                         op0=ALU.max, op1=ALU.min).then_inc(probs_ready, 1)

            def invert_sums(b):
                dve.wait_ge(acc_turned, b + 1)
                dve.tensor_scalar(iso[:, :], turned_den, 0.0, None, ALU.is_equal).then_inc(dve_epi, 1)
                dve.wait_ge(dve_epi, b * DVE_STEPS + ISO)
                dve.scalar_tensor_tensor(out=den[:, :], in0=iso[:, :], scalar=float(N), in1=turned_den,
                                         op0=ALU.mult, op1=ALU.add).then_inc(dve_epi, 1)
                dve.wait_ge(dve_epi, b * DVE_STEPS + NUM_ISO)
                dve.reciprocal(rden[:, :], den[:, :]).then_inc(dve_epi, 1)

            def attend(b):
                dve.wait_ge(dve_epi, b * DVE_STEPS + RDEN)
                dve.tensor_tensor(h[:, :, :], turned, over_cols(rden[:, :]), ALU.mult).then_inc(dve_epi, 1)
                dve.wait_ge(pool_epi, b * POOL_STEPS + H_ISO)
                dve.wait_ge(dve_epi, b * DVE_STEPS + H)
                dve.tensor_tensor(h[:, :, :], h[:, :, :], h_iso[:, :, :], ALU.add).then_inc(dve_epi, 1)
                dve.wait_ge(dve_epi, b * DVE_STEPS + H_ALL)
                dve.tensor_scalar(h_neg[:, :], h[:, :, :].rearrange("p t d -> p (t d)"), 0.0, None, ALU.min)\
                   .then_inc(dve_epi, 1)

            def add_residual(b):
                dve.wait_ge(act_epi, b * ACT_STEPS + ELU_EXP)
                dve.scalar_tensor_tensor(out=h_exp[:, :], in0=h_exp[:, :], scalar=-1.0, in1=xn_s[:, b, :],
                                         op0=ALU.add, op1=ALU.add).then_inc(dve_epi, 1)
                dve.wait_ge(dve_epi, b * DVE_STEPS + X_EXP)
                dve.scalar_tensor_tensor(out=res[:, :, :].rearrange("p t d -> p (t d)"),
                                         in0=h[:, :, :].rearrange("p t d -> p (t d)"), scalar=0.0,
                                         in1=h_exp[:, :], op0=ALU.max, op1=ALU.add).then_inc(dve_epi, 1)
                dve.wait_ge(dve_epi, b * DVE_STEPS + RES)
                dve.reduce_sum(row_sum[:, :], res[:, :, :], AX_X).then_inc(dve_epi, 1)
                dve.wait_ge(dve_epi, b * DVE_STEPS + ROW_SUM)
                dve.tensor_scalar(mean[:, :], row_sum[:, :], 1.0 / D, None, ALU.mult).then_inc(dve_epi, 1)

            def sum_squares(b):
                dve.wait_ge(pool_epi, b * POOL_STEPS + SQ)
                dve.reduce_sum(sq_sum[:, :], sq[:, :, :], AX_X).then_inc(dve_epi, 1)
                dve.wait_ge(dve_epi, b * DVE_STEPS + SQ_SUM)
                dve.tensor_scalar(var[:, :], sq_sum[:, :], 1.0 / D, EPS, ALU.mult, ALU.add).then_inc(dve_epi, 1)

            def r_arg(c):
                dve.wait_ge(f_ready, c + 1)
                b, at = c // CHUNKS, c % CHUNKS * CHUNK
                dve.tensor_scalar(r[:, b, at:at + CHUNK], ps[:, WH + c % FB, :], g_max[:, 0:1], 0.0,
                                  ALU.add, ALU.max).then_inc(r_arg_ready, 1)

            dve.wait_ge(wa_ready, 1)
            dve.wait_ge(consts_ready, 2)
            dve.tensor_copy(w_g[:, D:C], ps[:, ACC[0], 1:2]).then_inc(w_g_ready, 1)
            dve.tensor_scalar(wa1[:, :], ones[:, :], ps[:, ACC[0], 0:1], None, ALU.mult).then_inc(w_g_ready, 1)
            banks = sorted((wh_place(jt)[0], jt) for jt in range(JT))
            for n in range(2 * HALF_BANKS):
                tiles = [jt for bank, jt in banks if bank == WH + n]
                dve.wait_ge(wh_ready, n // HALF_BANKS + 1 + 2 * (n % HALF_BANKS))
                dve.tensor_copy(whg[:, tiles[0]:tiles[-1] + 1, :].rearrange("p t c -> p (t c)"),
                                ps[:, WH + n, 0:len(tiles) * C]).then_inc(whg_ready, 1)
            dve.wait_ge(whg_ready, 2 * HALF_BANKS)
            dve.reduce_max(g_edge[:, :], whg[:, :, D], AX_X).then_inc(edge_ready, 1)
            dve.wait_ge(edge_turned, 1)
            dve.reduce_max(g_top[:, :], ps[0:1, DEN[0], 0:P], AX_X).then_inc(top_ready, 1)
            dve.wait_ge(top_spread, 1)
            dve.tensor_copy(g_max[:, :], ps[:, DEN[0], P:P + 1]).then_inc(g_max_ready, 1)
            dve.wait_ge(g_max_ready, 1)
            dve.tensor_scalar(bias_f[:, :], g_max[:, :], -SLOPE, None, ALU.mult).then_inc(biases_ready, 1)
            dve.tensor_scalar(bias_q[:, :], g_max[:, :], -(1 - SLOPE), None, ALU.mult).then_inc(biases_ready, 1)
            for c in range(CHUNKS):
                r_arg(c)
            dve.wait_ge(factors_ready, 1)
            dve.tensor_scalar(raised_f[:, :], scale_f[:, :], RAISE, None, ALU.mult).then_inc(raised_ready, 1)
            dve.wait_ge(raised_ready, 1)
            dve.tensor_tensor(v[:, :, 0:D], whg[:, :, 0:D], over_cols(raised_f[:, :]), ALU.mult)\
               .then_inc(v_ready, 1)
            dve.wait_ge(factors_ready, 2)
            dve.wait_ge(x_sum_ready, 1)
            dve.tensor_scalar(x_sums[:, :], ones[:, :], x_sum[:, 0:1], None, ALU.mult).then_inc(x_sums_ready, 1)
            dve.wait_ge(r_ready, CHUNKS)
            for jt in range(JT):
                weights(0, jt, jt >= PROBS)
                if jt < FC - CHUNKS:
                    r_arg(CHUNKS + jt)
                if jt == FC + PROBS // 2:
                    dve.wait_ge(sum_wh_summed, 1)
                    dve.tensor_copy(sum_wh[:, :], ps[:, SUM_WH, 0:D]).then_inc(sum_wh_ready, 1)
            dve.wait_ge(xn_landed, 16)
            dve.wait_ge(r_ready, FC)
            with dve.Fori(1, BLOCKS) as b:
                for jt in range(JT):
                    weights(b, jt, True)
                    if jt == 13:
                        invert_sums(b - 1)
                    if jt == 15:
                        attend(b - 1)
                    if jt == 19:
                        add_residual(b - 1)
                    if jt == 24:
                        sum_squares(b - 1)
            invert_sums(BLOCKS - 1)
            attend(BLOCKS - 1)
            add_residual(BLOCKS - 1)
            sum_squares(BLOCKS - 1)

        @block.tensor
        def _(pe):
            pe.wait_ge(w_landed, 16 * 5)
            pe.matmul(ps[:, ACC[0], 0:2], wt_s[:, :], a_s[:, :], start=True, stop=True).then_inc(wa_ready, 1)
            pe.wait_ge(w_g_ready, 1)
            pe.wait_ge(xt_landed, 16)
            for at in range(JT // 2):
                for half in range(2):
                    bank, col = wh_place(half * (JT // 2) + at)
                    rows = slice(half * D, (half + 1) * D)
                    mm = pe.matmul(ps[:, bank, col:col + C], xt_s[rows, at * P:(at + 1) * P], w_g[rows, :],
                                   start=True, stop=True)
                    if at % PER_BANK == PER_BANK - 1 or at == JT // 2 - 1:
                        mm.then_inc(wh_ready, 1)
            pe.wait_ge(ident_ready, 1)
            pe.wait_ge(edge_ready, 1)
            pe.matmul(ps[0:1, DEN[0], 0:P], g_edge[:, :], ident[:, :], start=True, stop=True)\
              .then_inc(edge_turned, 1)
            pe.wait_ge(w_g_ready, 2)

            def f_chunk(c):
                if c >= FB:
                    pe.wait_ge(r_arg_ready, c - FB + 1)
                half, at = c // (FC // 2), c % (FC // 2) * CHUNK
                rows = slice(half * D, (half + 1) * D)
                pe.matmul(ps[:, WH + c % FB, :], wa1[rows, :], xt_s[rows, at:at + CHUNK],
                          start=True, stop=True).then_inc(f_ready, 1)

            f_chunk(0)
            pe.wait_ge(top_ready, 1)
            pe.matmul(ps[:, DEN[0], P:P + 1], ones[0:1, :], g_top[:, :], start=True, stop=True)\
              .then_inc(top_spread, 1)
            for c in range(1, FC):
                f_chunk(c)

            def add_pair(b, k):
                for parity in range(PAIR):
                    jt = PAIR * k + parity
                    pe.wait_ge(probs_ready, b * JT + jt + 1)
                    for c in range(CHUNKS):
                        for half in range(2):
                            to = (CHUNKS * c + half) * COLS
                            pe.matmul(ps[to:to + COLS, ACC[b % 2], :], v[:, jt, half * COLS:(half + 1) * COLS],
                                      probs[:, jt % PROBS, c * CHUNK:(c + 1) * CHUNK],
                                      start=(jt == 0), stop=(jt == JT - 1))
                for parity in range(PAIR):
                    jt = PAIR * k + parity
                    for c in range(CHUNKS):
                        to = (CHUNKS * parity + c) * COLS
                        mm = pe.matmul(ps[to:to + COLS, DEN[b % 2], :], v[:, jt, D:V],
                                       probs[:, jt % PROBS, c * CHUNK:(c + 1) * CHUNK],
                                       start=(k == 0), stop=(k == PAIRS - 1))
                mm.then_inc(probs_used, 1)

            def turn(b):
                pe.wait_ge(act_epi, b * ACT_STEPS + TAKE_DEN)
                if b >= 1:
                    pe.wait_ge(dve_epi, (b - 1) * DVE_STEPS + H)
                for t in range(TURNS):
                    pe.transpose(ps[:, TURN, t * P:(t + 1) * P], acc_s[:, t * P:(t + 1) * P], ident[:, :])
                pe.wait_ge(pick_steps, 2)
                for t in range(TURNS):
                    mm = pe.matmul(ps[:, TURN_DEN, t * CHUNKS:(t + 1) * CHUNKS], den_s[:, t * P:(t + 1) * P],
                                   pick[:, :], start=True, stop=True)
                mm.then_inc(acc_turned, 1)

            pe.wait_ge(v_ready, 1)
            pe.wait_ge(v_den_ready, 1)
            pe.wait_ge(g_max_ready, 1)
            for b in range(BLOCKS):
                if b == 1:
                    pe.wait_ge(r_arg_ready, FC)
                if b >= 2:
                    pe.wait_ge(act_epi, (b - 2) * ACT_STEPS + TAKE_DEN)
                for k in range(PAIRS):
                    add_pair(b, k)
                    if b == 0 and k == FC // PAIR:
                        pe.wait_ge(x_sums_ready, 1)
                        pe.wait_ge(r_arg_ready, FC)
                        pe.matmul(ps[:, SUM_WH, 0:D], x_sums[:, :], w_g[:, 0:D], start=True, stop=True)\
                          .then_inc(sum_wh_summed, 1)
                    if b >= 1 and k == 2:
                        turn(b - 1)
            turn(BLOCKS - 1)


def kernel(x, adj, L0_gnn_W, L0_gnn_a):
    import numpy as np
    import concourse.bacc as bacc
    from concourse.bass_utils import run_bass_kernel_spmd

    x, adj, W, a = (np.asarray(t) for t in (x, adj, L0_gnn_W, L0_gnn_a))
    N, D = x.shape
    B = N // BLOCK
    nodes = x.reshape(B, P, TURNS, CHUNKS, D)
    arrays = {
        "xt": np.ascontiguousarray(nodes.transpose(4, 0, 3, 2, 1).reshape(D, 2, N // 2).transpose(1, 0, 2)
                                   .reshape(2 * D, N // 2)),
        "xn": np.ascontiguousarray(x.reshape(B, P, TILES * D).transpose(1, 0, 2)),
        "w": np.ascontiguousarray(W),
        "wt": np.ascontiguousarray(W.T),
        "a": np.ascontiguousarray(a.reshape(2, D).T),
        "adj": np.ascontiguousarray(
            adj.reshape(B, P, TURNS, CHUNKS, B, P, TURNS // PAIR, PAIR, CHUNKS)
            .transpose(0, 4, 8, 6, 5, 7, 3, 2, 1)
        ).reshape(B, N // P // PAIR, P, PAIR * BLOCK),
    }
    nc = bacc.Bacc("TRN2", target_bir_lowering=False, num_devices=1)
    ins = {name: nc.dram_tensor(f"in_{name}", t.shape, mybir.dt.from_np(t.dtype), kind="ExternalInput").ap()
           for name, t in arrays.items()}
    out = nc.dram_tensor("out", (P, B, TILES * D), F32, kind="ExternalOutput").ap()
    gat_layer(nc, ins["xt"], ins["xn"], ins["w"], ins["wt"], ins["a"], ins["adj"], out)
    got = run_bass_kernel_spmd(nc, [{f"in_{name}": t for name, t in arrays.items()}], core_ids=[0])
    return got.results[0]["out"].transpose(1, 0, 2).reshape(N, D)
```

```python
import concourse.bass as bass
from concourse import mybir
from contextlib import ExitStack

F32 = mybir.dt.float32
BF16 = mybir.dt.bfloat16
I32 = mybir.dt.int32
ALU = mybir.AluOpType
ACT = mybir.ActivationFunctionType
AX_X = mybir.AxisListType.X

P = 128
SLOPE = 0.2
EPS = 1e-5

BLOCKS = 2
SQUARE = 32
QUARTERS = P // SQUARE
BANK = 512
BLOCK = QUARTERS * BANK
TILES = BLOCK // P
PART_TILES = (8, 8)
PARTS = len(PART_TILES)
RING = 8
MASKS = 4
PROBS = 4
SETS = ((0, 1, 2), (3, 4, 5))
SPARE = (6, 7)
HEAD = 2 * RING
AHEAD = 3
WARM = (5, 2)
LAST = 4
OWN = 4
F_AT = (2, 8)
R_AT = (6, 7, 11, 12)
CAP_AT = (7, 8, 12, 13)
SUM_WH_AT = 14
EPILOGUE_AT = ((3, 5, 9, 12, 14, 18, 24), (7, 10, 15, 17, 19, 20, 27))
EXP_AT = (10, 14)
SQ_AT = (22, 25)


def gat_layer(nc, xt, xn, weights_in, adj, out):
    D = 64
    N = 2 * xt.shape[1]
    LOADS = adj.shape[1]
    JT = LOADS
    JH = JT // 2
    V = D + SQUARE
    FC = N // BANK
    F_BANKS = (0, 1, 2, 3, 6, 3, 7, 6)
    WH_BANKS = (4, 5)
    CONSTS = 4
    SMALL = 3
    assert 2 * D == P and 2 * SQUARE == D and N == BLOCKS * BLOCK and FC == len(F_BANKS)
    assert LOADS % RING == 0 and RING % MASKS == 0 and RING % PROBS == 0 and LOADS > HEAD
    assert sum(PART_TILES) == TILES and PARTS == 2

    with ExitStack() as ctx:
        def sb(name, shape, dt=F32):
            return ctx.enter_context(nc.sbuf_tensor(name, shape, dt))

        def sem(name):
            return ctx.enter_context(nc.semaphore(name))

        xt_s = sb("xt_s", [P, N // 2])
        xn_s = sb("xn_s", [P, N // P * D])
        weights_s = sb("weights_s", [P, 2 * D + P + 2])
        w_s = (weights_s[:, 0:D], weights_s[:, D:2 * D])
        wt_s = weights_s[0:D, 2 * D:2 * D + P]
        a_s = weights_s[0:D, 2 * D + P:2 * D + P + 2]
        half_ones = sb("half_ones", [P, 2, P])
        wa1 = sb("wa1", [P, 2, P])
        wa2 = sb("wa2", [P, 2, SQUARE])
        x_sum = sb("x_sum", [P, 1])
        x_sums = sb("x_sums", [P, P])
        ones = sb("ones", [P, P])
        heads = sb("heads", [P, QUARTERS])
        g_edge = sb("g_edge", [P, 2])
        g_heads = sb("g_heads", [P, 2, QUARTERS])
        g_max = sb("g_max", [P, 1])
        bias_q = sb("bias_q", [P, 1])
        bias_f = sb("bias_f", [P, 1])
        gt = sb("gt", [P, JT, SQUARE])
        q = sb("q", [P, JT])
        v = sb("v", [P, JT, V])
        r = sb("r", [P, N])
        mean_wh = sb("mean_wh", [P, D])
        exp_wh = sb("exp_wh", [P, D])
        edgeless_elu = sb("edgeless_elu", [P, D])
        ring = sb("ring", [P, RING, BLOCK], I32)
        mask = sb("mask", [P, MASKS, BLOCK], BF16)
        probs = sb("probs", [P, PROBS, BLOCK])
        dev_try = sb("dev_try", [P, 1])
        dev = sb("dev", [P, PART_TILES[-1]])
        early_h = sb("early_h", [P, PART_TILES[-1], D])
        early_den = sb("early_den", [P, PART_TILES[-1], SQUARE])
        def by_part(name, *cols):
            return [sb(f"{name}{p}", [P, tiles, *cols]) for p, tiles in enumerate(PART_TILES)]

        h_s = by_part("h_s", D)
        den_s = by_part("den_s", SQUARE)
        iso = by_part("iso")
        den = by_part("den")
        rden = by_part("rden")
        xe_s = by_part("xe_s", D)
        exp_s = by_part("exp_s", D)
        res_s = by_part("res_s", D)
        row_sum = by_part("row_sum")
        mean = by_part("mean")
        cent_s = by_part("cent_s", D)
        sq_s = by_part("sq_s", D)
        sq_sum = by_part("sq_sum")
        var = by_part("var")
        minus_half = sb("minus_half", [P, TILES])
        rstd = by_part("rstd")

        ps = ctx.enter_context(nc.psum_tensor("ps", [P, 8, BANK], F32))

        w_landed = sem("w_landed")
        xt_landed = [sem(f"xt_landed{w}") for w in range(2)]
        xn_landed = [sem(f"xn_landed{b}") for b in range(BLOCKS)]
        adj_landed = [sem(f"adj_landed{s}") for s in range(RING)]
        first_landed = [sem(f"first_landed{c}") for c in range(1, QUARTERS)]
        consts_ready = sem("consts_ready")
        ones_ready = sem("ones_ready")
        heads_ready = sem("heads_ready")
        wa_ready = sem("wa_ready")
        wa2_ready = sem("wa2_ready")
        wa1_ready = sem("wa1_ready")
        g_ready = sem("g_ready")
        gt_ready = sem("gt_ready")
        wh_ready = sem("wh_ready")
        wh_turned = sem("wh_turned")
        edge_ready = sem("edge_ready")
        g_heads_ready = sem("g_heads_ready")
        g_heads_spread = sem("g_heads_spread")
        g_max_ready = sem("g_max_ready")
        biases_ready = sem("biases_ready")
        q_ready = sem("q_ready")
        v_den_ready = sem("v_den_ready")
        v_ready = sem("v_ready")
        v_rest_ready = sem("v_rest_ready")
        f_ready = sem("f_ready")
        r_exp = sem("r_exp")
        r_ready = sem("r_ready")
        x_sum_ready = sem("x_sum_ready")
        x_sums_ready = sem("x_sums_ready")
        sum_wh_summed = sem("sum_wh_summed")
        mean_wh_ready = sem("mean_wh_ready")
        exp_wh_ready = sem("exp_wh_ready")
        edgeless_steps = sem("edgeless_steps")
        mask_ready = sem("mask_ready")
        probs_ready = sem("probs_ready")
        probs_used = sem("probs_used")
        early_turned = sem("early_turned")
        dev_tried = sem("dev_tried")
        dev_ready = sem("dev_ready")
        inv_ready = sem("inv_ready")
        late_added = sem("late_added")
        dve_epi = [sem(f"dve_epi{p}") for p in range(PARTS)]
        pool_epi = [sem(f"pool_epi{p}") for p in range(PARTS)]
        h_exp_ready = [sem(f"h_exp_ready{p}") for p in range(PARTS)]
        centred = [sem(f"centred{p}") for p in range(PARTS)]
        sq_ready = [sem(f"sq_ready{p}") for p in range(PARTS)]
        y_ready = [sem(f"y_ready{p}") for p in range(PARTS)]
        y_stored = [sem(f"y_stored{p}") for p in range(PARTS)]

        TURN_DEN, ISO, DEN, RDEN, TURN_LOW, TURN_HIGH, H, X_H, RES, ROW_SUM, MEAN, SQ_SUM, VAR = range(1, 14)
        DVE_STEPS = VAR
        ISO_ELU, XE, RSTD = range(1, 4)
        POOL_STEPS = RSTD

        TOTAL = BLOCKS * LOADS
        LAST_FROM = TOTAL - LAST

        def last_parts():
            return [(LAST_FROM + p * LAST + i, LAST_FROM + i, p) for p in range(PARTS) for i in range(LAST)]

        LATE = (BLOCKS - 1, PARTS - 1)

        def through(n):
            return n + QUARTERS

        def part_cols(p):
            at = sum(PART_TILES[:p]) * SQUARE
            return slice(at, at + PART_TILES[p] * SQUARE)

        def part_of_load(buf, slot, p):
            return buf[:, slot, :].rearrange("p (c n) -> p c n", n=BANK)[:, :, part_cols(p)]

        def flat(buf, p):
            return buf[p][:, :, :].rearrange("p t d -> p (t d)")

        def over_cols(per_tile):
            return per_tile.unsqueeze(2).to_broadcast([P, per_tile.shape[1], D])

        def block_cols(b):
            return slice(b * TILES * D, (b + 1) * TILES * D)

        def x_cols(b, p):
            at = (b * TILES + sum(PART_TILES[:p])) * D
            return slice(at, at + PART_TILES[p] * D)

        adj_all = adj.rearrange("b n p i -> (b n) p i")
        adj_by_row = adj.rearrange("b n p i -> p (b n) i")
        block = ctx.enter_context(nc.Block())

        @block.sync
        def _(sp):
            sp.dma_start(weights_s[:, :], weights_in).then_inc(w_landed, 16)
            for w in range(2):
                cols = slice(w * N // 4, (w + 1) * N // 4)
                sp.dma_start(xt_s[:, cols], xt[:, cols]).then_inc(xt_landed[w], 16)
            for c in range(QUARTERS):
                cols = slice(c * BANK, (c + 1) * BANK)
                sp.dma_start(ring[:, 0, cols], adj[0, 0, :, cols])\
                  .then_inc(first_landed[c - 1] if c else adj_landed[0], 16)
            for k in range(1, RING):
                sp.dma_start(ring[:, k, :], adj[0, k]).then_inc(adj_landed[k], 16)
            sp.dma_start(xn_s[:, block_cols(0)], xn[:, block_cols(0)]).then_inc(xn_landed[0], 16)
            with sp.Fori(1, LAST_FROM // RING) as turn:
                for k in range(RING):
                    sp.wait_ge(mask_ready, through((turn - 1) * RING + k))
                    sp.dma_start(ring[:, k, :], adj_all[turn * RING + k]).then_inc(adj_landed[k], 16)
            for n in range(LAST_FROM // RING * RING, LAST_FROM):
                sp.wait_ge(mask_ready, through(n - RING))
                sp.dma_start(ring[:, n % RING, :], adj_all[n]).then_inc(adj_landed[n % RING], 16)
            for n, load, p in last_parts():
                sp.wait_ge(mask_ready, through(n - RING))
                sp.dma_start(part_of_load(ring, n % RING, p), part_of_load(adj_by_row, load, p))\
                  .then_inc(adj_landed[n % RING], 16)

            sp.dma_start(xn_s[:, block_cols(1)], xn[:, block_cols(1)]).then_inc(xn_landed[1], 16)
            for b in range(BLOCKS):
                for p in range(PARTS):
                    sp.wait_ge(y_ready[p], b + 1)
                    sp.dma_start(out[:, x_cols(b, p)], flat(cent_s, p)).then_inc(y_stored[p], 16)
            for p in range(PARTS):
                sp.wait_ge(y_stored[p], 16 * BLOCKS)

        @block.gpsimd
        def _(pool):
            pool.memset(ones[:, :], 1.0).then_inc(ones_ready, 1)
            pool.memset(half_ones[:, :, :], 0.0).then_inc(consts_ready, 1)
            pool.memset(minus_half[:, :], -0.5).then_inc(consts_ready, 1)
            pool.wait_ge(consts_ready, 2)
            pool.memset(half_ones[0:D, 0, :], 1.0).then_inc(consts_ready, 1)
            pool.wait_ge(consts_ready, 3)
            pool.memset(half_ones[D:P, 1, :], 1.0).then_inc(consts_ready, 1)
            pool.wait_ge(consts_ready, CONSTS)
            pool.wait_ge(ones_ready, 1)
            pool.affine_select(out=heads[:, :], in_=ones[:, 0:QUARTERS], compare_op=ALU.is_equal, fill=0.0, base=0,
                               pattern=[[-SQUARE, QUARTERS]], channel_multiplier=1).then_inc(heads_ready, 1)
            for half, tiles in enumerate((slice(OWN, JH), slice(JH, JT))):
                pool.wait_ge(v_den_ready, half + 1)
                pool.wait_ge(wh_turned, 2 * half + 2)
                pool.tensor_tensor(v[:, tiles, 0:D], v[:, tiles, 0:D],
                                   v[:, tiles, D:D + 1].to_broadcast([P, tiles.stop - tiles.start, D]),
                                   ALU.mult).then_inc(v_rest_ready, 1)

            def extend_x(b, p):
                if b:
                    pool.wait_ge(dve_epi[p], (b - 1) * DVE_STEPS + X_H)
                pool.wait_ge(dve_epi[p], b * DVE_STEPS + ISO)
                pool.tensor_tensor(xe_s[p][:, :, :], edgeless_elu[:, :].unsqueeze(1).to_broadcast([P, PART_TILES[p], D]),
                                   over_cols(iso[p][:, :]), ALU.mult).then_inc(pool_epi[p], 1)
                pool.wait_ge(pool_epi[p], b * POOL_STEPS + ISO_ELU)
                pool.tensor_tensor(flat(xe_s, p), flat(xe_s, p), xn_s[:, x_cols(b, p)], ALU.add)\
                    .then_inc(pool_epi[p], 1)

            def centre_rows(b, p):
                pool.wait_ge(dve_epi[p], b * DVE_STEPS + MEAN)
                pool.wait_ge(y_stored[p], 16 * b)
                pool.tensor_tensor(cent_s[p][:, :, :], res_s[p][:, :, :], over_cols(mean[p][:, :]), ALU.subtract)\
                    .then_inc(centred[p], 1)

            def invert_deviation(b, p):
                pool.wait_ge(dve_epi[p], b * DVE_STEPS + VAR)
                pool.tensor_tensor(rstd[p][:, :], var[p][:, :], minus_half[:, 0:PART_TILES[p]], ALU.pow).then_inc(pool_epi[p], 1)

            def scale_rows(b, p):
                pool.wait_ge(pool_epi[p], b * POOL_STEPS + RSTD)
                pool.tensor_tensor(cent_s[p][:, :, :], cent_s[p][:, :, :], over_cols(rstd[p][:, :]), ALU.mult)\
                    .then_inc(y_ready[p], 1)

            pool.wait_ge(edgeless_steps, 2)
            pool.wait_ge(xn_landed[0], 16)
            for p in range(PARTS):
                extend_x(0, p)
            for p in range(PARTS):
                invert_deviation(0, p)
                scale_rows(0, p)
            pool.wait_ge(xn_landed[1], 16)
            extend_x(1, 0)
            centre_rows(1, 0)
            extend_x(1, 1)
            invert_deviation(1, 0)
            scale_rows(1, 0)

        @block.scalar
        def _(act):
            def make_mask(n, slot, landed, slot_used):
                act.wait_ge(adj_landed[slot], 16 * landed)
                if slot_used:
                    act.wait_ge(probs_ready, through(n - MASKS))
                act.activation(mask[:, slot % MASKS, :], ring[:, slot, :], ACT.Relu).then_inc(mask_ready, 1)

            def make_first_mask(c):
                act.wait_ge(first_landed[c - 1] if c else adj_landed[0], 16)
                cols = slice(c * BANK, (c + 1) * BANK)
                act.activation(mask[:, 0, cols], ring[:, 0, cols], ACT.Relu).then_inc(mask_ready, 1)

            def make_part_mask(n, p):
                act.wait_ge(adj_landed[n % RING], 16 * (n // RING + 1))
                act.wait_ge(probs_ready, through(n - MASKS))
                act.activation(part_of_load(mask, n % MASKS, p), part_of_load(ring, n % RING, p), ACT.Relu)\
                   .then_inc(mask_ready, 1)

            def exp_h(b, p):
                act.wait_ge(dve_epi[p], b * DVE_STEPS + H)
                act.activation(flat(exp_s, p), flat(h_s, p), ACT.Exp).then_inc(h_exp_ready[p], 1)

            def square(b, p):
                act.wait_ge(centred[p], b + 1)
                act.activation(flat(sq_s, p), flat(cent_s, p), ACT.Square).then_inc(sq_ready[p], 1)

            def r_chunk(c):
                act.wait_ge(f_ready, c + 1)
                act.activation(r[:, c * BANK:(c + 1) * BANK], ps[:, F_BANKS[c], :], ACT.Exp,
                               bias=bias_q[:, :], scale=-(1 - SLOPE)).then_inc(r_exp, 1)

            def exp_q(half):
                tiles = slice(half * JH, (half + 1) * JH)
                act.wait_ge(gt_ready, half + 1)
                act.activation(q[:, tiles], gt[:, tiles, 0], ACT.Exp, bias=bias_q[:, :], scale=1 - SLOPE)\
                   .then_inc(q_ready, 1)

            def exp_f(half):
                tiles = slice(half * JH, (half + 1) * JH)
                act.activation(v[:, tiles, D:V], gt[:, tiles, :], ACT.Exp, bias=bias_f[:, :], scale=SLOPE)\
                   .then_inc(v_den_ready, 1)

            for c in range(QUARTERS - 1):
                make_first_mask(c)
            act.wait_ge(biases_ready, 2)
            exp_q(0)
            r_chunk(0)
            exp_f(0)
            for c in range(1, FC // 2):
                r_chunk(c)
            make_first_mask(QUARTERS - 1)
            for k in range(1, HEAD):
                make_mask(k, k % RING, k // RING + 1, k >= MASKS)
                if k == 2:
                    exp_q(1)
                    exp_f(1)
                if k == 3:
                    act.wait_ge(xt_landed[0], 16)
                    act.wait_ge(xt_landed[1], 16)
                    act.activation(r[:, N // 2:N], xt_s[:, :], ACT.Copy, accum_out=x_sum[:, :])\
                       .then_inc(x_sum_ready, 1)
                if k in R_AT:
                    act.wait_ge(x_sum_ready, 1)
                    r_chunk(FC // 2 + R_AT.index(k))
            with act.Fori(HEAD // RING, LOADS // RING) as turn:
                for k in range(RING):
                    make_mask(turn * RING + k, k, turn + 1, True)
            act.wait_ge(mean_wh_ready, 2)
            act.activation(exp_wh[:, :], exp_wh[:, :], ACT.Exp).then_inc(exp_wh_ready, 1)
            for k in range(LOADS - LAST):
                n = LOADS + k
                make_mask(n, n % RING, n // RING + 1, True)
                for p in range(PARTS):
                    if k == EXP_AT[p]:
                        exp_h(0, p)
                    if k == SQ_AT[p]:
                        square(0, p)
            for n, load, p in last_parts():
                make_part_mask(n, p)
            exp_h(1, 0)
            square(1, 0)
            exp_h(1, 1)
            act.wait_ge(ones_ready, 1)
            act.activation(dev_try[:, :], ones[:, 0:1], ACT.Sqrt).then_inc(dev_tried, 1)
            square(1, 1)
            act.wait_ge(dve_epi[1], DVE_STEPS + VAR)
            act.activation(dev[:, :], var[1][:, :], ACT.Sqrt).then_inc(dev_ready, 1)
        @block.vector
        def _(dve):
            r_blocks = r[:, :].rearrange("p (b i) -> p b i", i=BLOCK)

            def weights(b, n, slot, jt, slot_used):
                dve.wait_ge(mask_ready, through(n))
                if slot_used:
                    dve.wait_ge(probs_used, n - PROBS + 1)
                dve.scalar_tensor_tensor(out=probs[:, slot % PROBS, :], in0=r[:, b * BLOCK:(b + 1) * BLOCK],
                                         scalar=q[:, bass.ds(jt, 1)], in1=mask[:, slot % MASKS, :],
                                         op0=ALU.max, op1=ALU.min).then_inc(probs_ready, 1)

            def first_weights(c):
                dve.wait_ge(mask_ready, c + 1)
                dve.wait_ge(r_ready, c + 1)
                cols = slice(c * BANK, (c + 1) * BANK)
                dve.scalar_tensor_tensor(out=probs[:, 0, cols], in0=r[:, cols], scalar=q[:, 0:1],
                                         in1=mask[:, 0, cols], op0=ALU.max, op1=ALU.min).then_inc(probs_ready, 1)

            def part_weights(n, load, p):
                dve.wait_ge(mask_ready, through(n))
                dve.wait_ge(probs_used, n - PROBS + 1)
                dve.scalar_tensor_tensor(out=part_of_load(probs, n % PROBS, p),
                                         in0=part_of_load(r_blocks, BLOCKS - 1, p),
                                         scalar=q[:, load - LOADS:load - LOADS + 1],
                                         in1=part_of_load(mask, n % MASKS, p),
                                         op0=ALU.max, op1=ALU.min).then_inc(probs_ready, 1)

            def squares(b, p, sums, late=False):
                return ps[:, SETS[0 if late else b][sums], part_cols(p)]\
                    .rearrange("p (t s) -> p t s", s=SQUARE)

            def turn_weight_sums(b, p):
                past = b * DVE_STEPS
                dve.wait_ge(probs_used, LOADS if b == 0 else TOTAL + p * LAST)
                late = (b, p) == LATE
                dve.transpose(den_s[p][:, :, :], squares(b, p, 2, late)).then_inc(dve_epi[p], 1)
                dve.wait_ge(dve_epi[p], past + TURN_DEN)
                if late:
                    dve.wait_ge(early_turned, 3)
                    dve.tensor_tensor(den_s[p][:, :, 0], den_s[p][:, :, 0], early_den[:, :, 0], ALU.add)\
                       .then_inc(late_added, 1)
                    dve.wait_ge(late_added, 1)
                dve.tensor_scalar(iso[p][:, :], den_s[p][:, :, 0], 0.0, None, ALU.is_equal)\
                   .then_inc(dve_epi[p], 1)
                dve.wait_ge(dve_epi[p], past + ISO)
                dve.tensor_tensor(den[p][:, :], iso[p][:, :], den_s[p][:, :, 0], ALU.add).then_inc(dve_epi[p], 1)
                dve.wait_ge(dve_epi[p], past + DEN)
                dve.reciprocal(rden[p][:, :], den[p][:, :]).then_inc(dve_epi[p], 1)

            def turn_early():
                b, p = LATE
                dve.wait_ge(probs_used, TOTAL)
                dve.transpose(early_den[:, :, :], squares(b, p, 2)).then_inc(early_turned, 1)
                dve.transpose(early_h[:, :, 0:SQUARE], squares(b, p, 0)).then_inc(early_turned, 1)
                dve.transpose(early_h[:, :, SQUARE:D], squares(b, p, 1)).then_inc(early_turned, 1)

            def attend(b, p):
                past = b * DVE_STEPS
                late = (b, p) == LATE
                dve.transpose(h_s[p][:, :, 0:SQUARE], squares(b, p, 0, late)).then_inc(dve_epi[p], 1)
                dve.transpose(h_s[p][:, :, SQUARE:D], squares(b, p, 1, late)).then_inc(dve_epi[p], 1)
                dve.wait_ge(dve_epi[p], past + TURN_HIGH)
                if late:
                    dve.tensor_tensor(flat(h_s, p), flat(h_s, p), early_h[:, :, :].rearrange("p t d -> p (t d)"),
                                      ALU.add).then_inc(late_added, 1)
                    dve.wait_ge(late_added, 2)
                dve.tensor_tensor(h_s[p][:, :, :], h_s[p][:, :, :], over_cols(rden[p][:, :]), ALU.mult)\
                   .then_inc(dve_epi[p], 1)

            def add_h(b, p):
                dve.wait_ge(dve_epi[p], b * DVE_STEPS + H)
                dve.wait_ge(pool_epi[p], b * POOL_STEPS + XE)
                dve.scalar_tensor_tensor(out=flat(res_s, p), in0=flat(h_s, p), scalar=0.0, in1=flat(xe_s, p),
                                         op0=ALU.max, op1=ALU.add).then_inc(dve_epi[p], 1)

            def add_exp(b, p):
                dve.wait_ge(dve_epi[p], b * DVE_STEPS + X_H)
                dve.wait_ge(h_exp_ready[p], b + 1)
                dve.scalar_tensor_tensor(out=flat(res_s, p), in0=flat(exp_s, p), scalar=1.0, in1=flat(res_s, p),
                                         op0=ALU.min, op1=ALU.add).then_inc(dve_epi[p], 1)

            def average(b, p):
                dve.wait_ge(dve_epi[p], b * DVE_STEPS + RES)
                dve.reduce_sum(row_sum[p][:, :], res_s[p][:, :, :], AX_X).then_inc(dve_epi[p], 1)
                dve.wait_ge(dve_epi[p], b * DVE_STEPS + ROW_SUM)
                dve.tensor_scalar(mean[p][:, :], row_sum[p][:, :], 1.0 / D, None, ALU.mult)\
                   .then_inc(dve_epi[p], 1)

            def centre(b, p):
                dve.wait_ge(dve_epi[p], b * DVE_STEPS + MEAN)
                if b:
                    dve.wait_ge(y_stored[p], 16 * b)
                dve.tensor_tensor(cent_s[p][:, :, :], res_s[p][:, :, :], over_cols(mean[p][:, :]), ALU.subtract)\
                   .then_inc(centred[p], 1)

            def sum_squares(b, p):
                dve.wait_ge(sq_ready[p], b + 1)
                dve.reduce_sum(sq_sum[p][:, :], sq_s[p][:, :, :], AX_X).then_inc(dve_epi[p], 1)
                dve.wait_ge(dve_epi[p], b * DVE_STEPS + SQ_SUM)
                dve.tensor_scalar(var[p][:, :], sq_sum[p][:, :], 1.0 / D, EPS, ALU.mult, ALU.add)\
                   .then_inc(dve_epi[p], 1)

            def scale_rows(b, p):
                dve.wait_ge(dev_ready, 1)
                dve.reciprocal(rstd[p][:, :], dev[:, :]).then_inc(inv_ready, 1)
                dve.wait_ge(inv_ready, 1)
                dve.tensor_tensor(cent_s[p][:, :, :], cent_s[p][:, :, :], over_cols(rstd[p][:, :]), ALU.mult)\
                   .then_inc(y_ready[p], 1)

            def cap_r(c):
                dve.wait_ge(r_exp, c + 1)
                cols = slice(c * BANK, (c + 1) * BANK)
                dve.tensor_scalar(r[:, cols], r[:, cols], 1.0, None, ALU.min).then_inc(r_ready, 1)

            def turn_wh(half, part):
                dve.wait_ge(wh_ready, 2 * half + part + 1)
                dve.transpose(v[:, half * JH:(half + 1) * JH, part * SQUARE:(part + 1) * SQUARE],
                              ps[:, WH_BANKS[part], :].rearrange("p (t s) -> p t s", s=SQUARE))\
                   .then_inc(wh_turned, 1)

            dve.wait_ge(wa_ready, 1)
            dve.wait_ge(consts_ready, CONSTS)
            dve.tensor_scalar(wa2[:, :, :], half_ones[:, :, 0:SQUARE], ps[:, SMALL, 1:2], None, ALU.mult)\
               .then_inc(wa2_ready, 1)
            dve.tensor_scalar(wa1[:, :, :], half_ones[:, :, :], ps[:, SMALL, 0:1], None, ALU.mult)\
               .then_inc(wa1_ready, 1)
            def find_edge(half):
                dve.wait_ge(g_ready, half + 1)
                dve.reduce_max(g_edge[:, half:half + 1], ps[:, SPARE[half], :], AX_X).then_inc(edge_ready, 1)
                dve.wait_ge(edge_ready, half + 1)
                dve.tensor_scalar(g_heads[:, half, :], heads[:, :], g_edge[:, half:half + 1], None, ALU.mult)\
                   .then_inc(g_heads_ready, 1)

            def turn_g(half):
                dve.transpose(gt[:, half * JH:(half + 1) * JH, :],
                              ps[:, SPARE[half], :].rearrange("p (t s) -> p t s", s=SQUARE)).then_inc(gt_ready, 1)

            dve.wait_ge(heads_ready, 1)
            dve.wait_ge(ones_ready, 1)
            find_edge(0)
            turn_g(0)
            turn_wh(0, 0)
            find_edge(1)
            dve.wait_ge(g_heads_spread, 1)
            dve.reduce_max(g_max[:, :], ps[:, SMALL, 0:2 * QUARTERS], AX_X).then_inc(g_max_ready, 1)
            dve.wait_ge(g_max_ready, 1)
            dve.tensor_scalar(bias_q[:, :], g_max[:, :], -(1 - SLOPE), None, ALU.mult).then_inc(biases_ready, 1)
            dve.tensor_scalar(bias_f[:, :], g_max[:, :], -SLOPE, None, ALU.mult).then_inc(biases_ready, 1)
            turn_wh(0, 1)
            cap_r(0)
            dve.wait_ge(v_den_ready, 1)
            dve.wait_ge(wh_turned, 2)
            dve.tensor_tensor(v[:, 0:OWN, 0:D], v[:, 0:OWN, 0:D], v[:, 0:OWN, D:D + 1].to_broadcast([P, OWN, D]),
                              ALU.mult).then_inc(v_ready, 1)
            dve.wait_ge(q_ready, 1)
            for c in range(QUARTERS):
                if c < QUARTERS - 1:
                    cap_r(c + 1)
                first_weights(c)
            for k in range(1, HEAD):
                weights(0, k, k, k, k >= PROBS)
                if k == 1:
                    turn_g(1)
                if k == 2:
                    turn_wh(1, 0)
                if k == 3:
                    turn_wh(1, 1)
                if k == 4:
                    dve.wait_ge(x_sum_ready, 1)
                    dve.tensor_scalar(x_sums[:, :], ones[:, :], x_sum[:, 0:1], None, ALU.mult)\
                       .then_inc(x_sums_ready, 1)
                if k in CAP_AT:
                    cap_r(FC // 2 + CAP_AT.index(k))
            dve.wait_ge(q_ready, 2)
            with dve.Fori(HEAD // RING, LOADS // RING) as turn:
                for k in range(RING):
                    weights(0, turn * RING + k, k, turn * RING + k, True)
            dve.wait_ge(sum_wh_summed, 1)
            dve.tensor_scalar(mean_wh[:, :], ps[:, SPARE[0], 0:D], 1.0 / N, None, ALU.mult)\
               .then_inc(mean_wh_ready, 1)
            dve.tensor_scalar(exp_wh[:, :], ps[:, SPARE[0], 0:D], 1.0 / N, 0.0, ALU.mult, ALU.min)\
               .then_inc(mean_wh_ready, 1)
            dve.wait_ge(r_ready, FC)
            steps = (turn_weight_sums, attend, add_h, add_exp, average, centre, sum_squares)
            for k in range(LOADS - LAST):
                n = LOADS + k
                weights(1, n, n % RING, k, True)
                if k == 1:
                    dve.wait_ge(exp_wh_ready, 1)
                    dve.tensor_scalar(exp_wh[:, :], exp_wh[:, :], -1.0, None, ALU.add)\
                       .then_inc(edgeless_steps, 1)
                    dve.wait_ge(edgeless_steps, 1)
                    dve.wait_ge(mean_wh_ready, 2)
                    dve.scalar_tensor_tensor(out=edgeless_elu[:, :], in0=mean_wh[:, :], scalar=0.0,
                                             in1=exp_wh[:, :], op0=ALU.max, op1=ALU.add)\
                       .then_inc(edgeless_steps, 1)
                for p in range(PARTS):
                    if k in EPILOGUE_AT[p]:
                        steps[EPILOGUE_AT[p].index(k)](0, p)
            parts = last_parts()
            for numbers in parts[:LAST + AHEAD]:
                part_weights(*numbers)
            turn_weight_sums(1, 0)
            for numbers in parts[LAST + AHEAD:]:
                part_weights(*numbers)
            attend(1, 0)
            turn_early()
            add_h(1, 0)
            add_exp(1, 0)
            average(1, 0)
            turn_weight_sums(1, 1)
            attend(1, 1)
            sum_squares(1, 0)
            add_h(1, 1)
            add_exp(1, 1)
            average(1, 1)
            centre(1, 1)
            sum_squares(1, 1)
            scale_rows(1, 1)

        @block.tensor
        def _(pe):
            def quarter(c):
                return slice(c * SQUARE, (c + 1) * SQUARE)

            pe.wait_ge(ones_ready, 1)
            for _ in range(WARM[0]):
                pe.matmul(ps[:, 0, 0:P], ones[:, :], ones[:, :], start=True, stop=True)
            pe.wait_ge(w_landed, 16)
            pe.matmul(ps[:, SMALL, 0:2], wt_s, a_s, start=True, stop=True).then_inc(wa_ready, 1)

            def make_g(half):
                pe.wait_ge(xt_landed[half], 16)
                for b in range(2):
                    for c in range(2):
                        at = (half * 2 + c) * BANK
                        mm = pe.matmul(ps[quarter(b * 2 + c), SPARE[half], :], wa2[:, b, :], xt_s[:, at:at + BANK],
                                       start=True, stop=True)
                mm.then_inc(g_ready, 1)

            def make_wh(half, part):
                for b in range(2):
                    for c in range(2):
                        at = (half * 2 + c) * BANK
                        mm = pe.matmul(ps[quarter(b * 2 + c), WH_BANKS[part], :], w_s[b][:, quarter(part)],
                                       xt_s[:, at:at + BANK], start=True, stop=True)
                mm.then_inc(wh_ready, 1)

            def make_f(c):
                half, at = c // (FC // 2), c % (FC // 2) * BANK
                pe.matmul(ps[:, F_BANKS[c], :], wa1[:, half, :], xt_s[:, at:at + BANK],
                          start=True, stop=True).then_inc(f_ready, 1)

            for _ in range(WARM[1]):
                pe.matmul(ps[:, 0, 0:P], ones[:, :], ones[:, :], start=True, stop=True)
            pe.wait_ge(wa2_ready, 1)
            make_g(0)
            make_wh(0, 0)
            make_g(1)
            make_wh(0, 1)
            pe.wait_ge(wa1_ready, 1)
            pe.wait_ge(g_heads_ready, 2)
            pe.matmul(ps[:, SMALL, 0:2 * QUARTERS], ones[:, :], g_heads[:, :, :].rearrange("p u c -> p (u c)"),
                      start=True, stop=True).then_inc(g_heads_spread, 1)
            make_f(0)
            make_f(1)
            make_f(2)
            pe.wait_ge(g_max_ready, 1)
            make_f(3)
            pe.wait_ge(wh_turned, 2)
            make_wh(1, 0)
            make_wh(1, 1)
            pe.wait_ge(gt_ready, 1)
            make_f(4)
            pe.wait_ge(r_exp, 4)
            make_f(5)

            def add_load(b, jt):
                n = b * LOADS + jt
                pe.wait_ge(probs_ready, through(n))
                for part in range(V // SQUARE):
                    for c in range(QUARTERS):
                        mm = pe.matmul(ps[quarter(c), SETS[b][part], :], v[:, jt, quarter(part)],
                                       probs[:, n % PROBS, c * BANK:(c + 1) * BANK],
                                       start=(jt == 0), stop=(jt == JT - 1))
                mm.then_inc(probs_used, 1)

            def add_part(n, load, p):
                b, jt = load // LOADS, load % LOADS
                weights = part_of_load(probs, n % PROBS, p)
                pe.wait_ge(probs_ready, through(n))
                for part in range(V // SQUARE):
                    for c in range(QUARTERS):
                        mm = pe.matmul(ps[quarter(c), SETS[b - p][part], part_cols(p)],
                                       v[:, jt, quarter(part)], weights[:, c, :],
                                       start=(p == 1 and load == LAST_FROM), stop=(load == TOTAL - 1))
                mm.then_inc(probs_used, 1)

            pe.wait_ge(v_ready, 1)
            for jt in range(JT):
                if jt == OWN:
                    pe.wait_ge(v_rest_ready, 1)
                if jt == JH:
                    pe.wait_ge(v_rest_ready, 2)
                add_load(0, jt)
                if jt == F_AT[0]:
                    pe.wait_ge(gt_ready, 2)
                    make_f(6)
                if jt == F_AT[1]:
                    pe.wait_ge(r_exp, 5)
                    make_f(7)
                if jt == SUM_WH_AT:
                    pe.wait_ge(x_sums_ready, 1)
                    pe.wait_ge(r_exp, FC)
                    pe.matmul(ps[:, SPARE[0], 0:D], x_sums[:, :], w_s[0], start=True, stop=False)
                    pe.matmul(ps[:, SPARE[0], 0:D], x_sums[:, :], w_s[1], start=False, stop=True)\
                      .then_inc(sum_wh_summed, 1)
            for jt in range(JT - LAST):
                add_load(1, jt)
            for n, load, p in last_parts():
                add_part(n, load, p)


def kernel(x, adj, L0_gnn_W, L0_gnn_a):
    import numpy as np
    import concourse.bacc as bacc
    from concourse.bass_utils import run_bass_kernel_spmd

    x, adj, W, a = (np.asarray(t) for t in (x, adj, L0_gnn_W, L0_gnn_a))
    N, D = x.shape
    order = np.arange(N).reshape(BLOCKS, QUARTERS, SQUARE, TILES).transpose(0, 1, 3, 2)
    j_order = order.reshape(BLOCKS, 2, 2, TILES, SQUARE).transpose(1, 3, 0, 2, 4).ravel()
    order = order.ravel()
    adj_rows = np.ascontiguousarray(adj.T)[j_order][:, order]
    arrays = {
        "xt": np.ascontiguousarray(x[order].T.reshape(D, 2, N // 2).transpose(1, 0, 2)).reshape(2 * D, N // 2),
        "xn": np.ascontiguousarray(x.reshape(BLOCKS, P, TILES * D).transpose(1, 0, 2)).reshape(P, N // P * D),
        "weights": np.concatenate([np.pad(W, ((0, D), (0, 0))), np.pad(W, ((D, 0), (0, 0))),
                                   np.tile(W.T, (2, 2)), np.tile(a.reshape(2, D).T, (2, 1))], axis=1),
        "adj": np.ascontiguousarray(adj_rows.reshape(N // P, P, BLOCKS, BLOCK).transpose(2, 0, 1, 3)),
    }
    nc = bacc.Bacc("TRN2", target_bir_lowering=False, num_devices=1)
    ins = {name: nc.dram_tensor(f"in_{name}", t.shape, mybir.dt.from_np(t.dtype), kind="ExternalInput").ap()
           for name, t in arrays.items()}
    out = nc.dram_tensor("out", (P, N // P * D), F32, kind="ExternalOutput").ap()
    gat_layer(nc, ins["xt"], ins["xn"], ins["weights"], ins["adj"], out)
    got = run_bass_kernel_spmd(nc, [{f"in_{name}": t for name, t in arrays.items()}], core_ids=[0])
    y = got.results[0]["out"]
    return y.reshape(P, BLOCKS, TILES, D).transpose(1, 0, 2, 3).reshape(N, D)
```

```python
import concourse.bass as bass
from concourse import mybir
from contextlib import ExitStack

F32 = mybir.dt.float32
BF16 = mybir.dt.bfloat16
I32 = mybir.dt.int32
ALU = mybir.AluOpType
ACT = mybir.ActivationFunctionType
AX_X = mybir.AxisListType.X

P = 128
SLOPE = 0.2
EPS = 1e-5

BLOCKS = 2
SQUARE = 32
QUARTERS = P // SQUARE
BANK = 512
BLOCK = QUARTERS * BANK
TILES = BLOCK // P
PART_TILES = (8, 4, 4)
PARTS = len(PART_TILES)
PIECES = ((0,), (1, 2))
RING = 8
MASKS = 4
PROBS = 4
SETS = ((0, 1, 2), (3, 4, 5))
SPARE = (6, 7)
HEAD = 2 * RING
LAST = 4
AHEAD = 3
WARM = (5, 2)
OWN = 4
F_AT = (2, 8)
R_AT = (6, 7, 11, 12)
CAP_AT = (7, 8, 12, 13)
SUM_WH_AT = 14
EPILOGUE_AT = ((3, 5, 9, 12, 14, 17, 23), (6, 8, 13, 15, 18, 20, 25), (7, 10, 16, 19, 21, 22, 27))
EXP_AT = (10, 13, 15)
SQ_AT = (21, 24, 25)


def gat_layer(nc, xt, xn, weights_in, adj, out):
    D = 64
    N = 2 * xt.shape[1]
    LOADS = adj.shape[1]
    JT = LOADS
    JH = JT // 2
    V = D + SQUARE
    FC = N // BANK
    F_BANKS = (0, 1, 2, 3, 6, 3, 7, 6)
    WH_BANKS = (4, 5)
    CONSTS = 5
    LATE_TILES = sum(PART_TILES[p] for p in PIECES[1])
    SMALL = 3
    assert 2 * D == P and 2 * SQUARE == D and N == BLOCKS * BLOCK and FC == len(F_BANKS)
    assert LOADS % RING == 0 and RING % MASKS == 0 and RING % PROBS == 0 and LOADS > HEAD
    assert sum(PART_TILES) == TILES and PARTS == 3 and len(PIECES) == 2

    with ExitStack() as ctx:
        def sb(name, shape, dt=F32):
            return ctx.enter_context(nc.sbuf_tensor(name, shape, dt))

        def sem(name):
            return ctx.enter_context(nc.semaphore(name))

        xt_s = sb("xt_s", [P, N // 2])
        xn_s = sb("xn_s", [P, N // P * D])
        weights_s = sb("weights_s", [P, 2 * D + P + 2])
        w_s = (weights_s[:, 0:D], weights_s[:, D:2 * D])
        wt_s = weights_s[0:D, 2 * D:2 * D + P]
        a_s = weights_s[0:D, 2 * D + P:2 * D + P + 2]
        half_ones = sb("half_ones", [P, 2, P])
        wa1 = sb("wa1", [P, 2, P])
        wa2 = sb("wa2", [P, 2, SQUARE])
        x_sum = sb("x_sum", [P, 1])
        x_sums = sb("x_sums", [P, P])
        ones = sb("ones", [P, P])
        minus_half = sb("minus_half", [P, TILES])
        eps_s = sb("eps_s", [P, 1])
        heads = sb("heads", [P, QUARTERS])
        g_edge = sb("g_edge", [P, 2])
        g_heads = sb("g_heads", [P, 2, QUARTERS])
        g_max = sb("g_max", [P, 1])
        bias_q = sb("bias_q", [P, 1])
        bias_f = sb("bias_f", [P, 1])
        gt = sb("gt", [P, JT, SQUARE])
        q = sb("q", [P, JT])
        v = sb("v", [P, JT, V])
        r = sb("r", [P, N])
        mean_wh = sb("mean_wh", [P, D])
        exp_wh = sb("exp_wh", [P, D])
        edgeless_elu = sb("edgeless_elu", [P, D])
        ring = sb("ring", [P, RING, BLOCK], I32)
        mask = sb("mask", [P, MASKS, BLOCK], BF16)
        probs = sb("probs", [P, PROBS, BLOCK])
        sqrt_unread = sb("sqrt_unread", [P, 1])
        early_h = sb("early_h", [P, LATE_TILES, D])
        early_den = sb("early_den", [P, LATE_TILES, SQUARE])

        def by_part(name, *cols):
            return [sb(f"{name}{p}", [P, tiles, *cols]) for p, tiles in enumerate(PART_TILES)]

        h_s = by_part("h_s", D)
        den_s = by_part("den_s", SQUARE)
        iso = by_part("iso")
        den = by_part("den")
        rden = by_part("rden")
        xe_s = by_part("xe_s", D)
        exp_s = by_part("exp_s", D)
        res_s = by_part("res_s", D)
        row_sum = by_part("row_sum")
        mean = by_part("mean")
        cent_s = by_part("cent_s", D)
        sq_s = by_part("sq_s", D)
        sq_sum = by_part("sq_sum")
        var = by_part("var")
        dev = by_part("dev")
        rstd = by_part("rstd")

        ps = ctx.enter_context(nc.psum_tensor("ps", [P, 8, BANK], F32))

        w_landed = sem("w_landed")
        xt_landed = [sem(f"xt_landed{w}") for w in range(2)]
        xn_landed = [sem(f"xn_landed{b}") for b in range(BLOCKS)]
        adj_landed = [sem(f"adj_landed{s}") for s in range(RING)]
        first_landed = [sem(f"first_landed{c}") for c in range(1, QUARTERS)]
        consts_ready = sem("consts_ready")
        ones_ready = sem("ones_ready")
        heads_ready = sem("heads_ready")
        wa_ready = sem("wa_ready")
        wa2_ready = sem("wa2_ready")
        wa1_ready = sem("wa1_ready")
        g_ready = sem("g_ready")
        gt_ready = sem("gt_ready")
        wh_ready = sem("wh_ready")
        wh_turned = sem("wh_turned")
        edge_ready = sem("edge_ready")
        g_heads_ready = sem("g_heads_ready")
        g_heads_spread = sem("g_heads_spread")
        g_max_ready = sem("g_max_ready")
        biases_ready = sem("biases_ready")
        q_ready = sem("q_ready")
        v_den_ready = sem("v_den_ready")
        v_ready = sem("v_ready")
        v_rest_ready = sem("v_rest_ready")
        f_ready = sem("f_ready")
        r_exp = sem("r_exp")
        r_ready = sem("r_ready")
        x_sum_ready = sem("x_sum_ready")
        x_sums_ready = sem("x_sums_ready")
        sum_wh_summed = sem("sum_wh_summed")
        mean_wh_ready = sem("mean_wh_ready")
        exp_wh_ready = sem("exp_wh_ready")
        edgeless_steps = sem("edgeless_steps")
        mask_ready = sem("mask_ready")
        probs_ready = sem("probs_ready")
        probs_used = sem("probs_used")
        early_turned = sem("early_turned")
        sqrt_loaded = sem("sqrt_loaded")
        dve_epi = [sem(f"dve_epi{p}") for p in range(PARTS)]
        pool_epi = [sem(f"pool_epi{p}") for p in range(PARTS)]
        late_added = [sem(f"late_added{p}") for p in range(PARTS)]
        dev_ready = [sem(f"dev_ready{p}") for p in range(PARTS)]
        rstd_ready = [sem(f"rstd_ready{p}") for p in range(PARTS)]
        h_exp_ready = [sem(f"h_exp_ready{p}") for p in range(PARTS)]
        centred = [sem(f"centred{p}") for p in range(PARTS)]
        sq_ready = [sem(f"sq_ready{p}") for p in range(PARTS)]
        y_ready = [sem(f"y_ready{p}") for p in range(PARTS)]
        y_stored = [sem(f"y_stored{p}") for p in range(PARTS)]

        TURN_DEN, TURN_LOW, TURN_HIGH, ISO, DEN, RDEN, H, X_H, RES, ROW_SUM, MEAN, SQ_SUM, VAR = range(1, 14)
        DVE_STEPS = VAR
        ISO_ELU, XE, RSTD = range(1, 4)
        POOL_STEPS = RSTD

        TOTAL = BLOCKS * LOADS
        LAST_FROM = TOTAL - LAST

        def through(n):
            return n + QUARTERS

        def last_pieces():
            return [(LAST_FROM + piece * LAST + i, LAST_FROM + i, piece)
                    for piece in range(len(PIECES)) for i in range(LAST)]

        def is_late(b, p):
            return b == BLOCKS - 1 and p in PIECES[1]

        def cols_of(parts):
            at = sum(PART_TILES[:parts[0]])
            return slice(at * SQUARE, (at + sum(PART_TILES[p] for p in parts)) * SQUARE)

        def piece_of(buf, slot, piece):
            return buf[:, slot, :].rearrange("p (c n) -> p c n", n=BANK)[:, :, cols_of(PIECES[piece])]

        def flat(buf, p):
            return buf[p][:, :, :].rearrange("p t d -> p (t d)")

        def over_cols(per_tile):
            return per_tile.unsqueeze(2).to_broadcast([P, per_tile.shape[1], D])

        def block_cols(b):
            return slice(b * TILES * D, (b + 1) * TILES * D)

        def x_cols(b, p):
            at = (b * TILES + sum(PART_TILES[:p])) * D
            return slice(at, at + PART_TILES[p] * D)

        adj_all = adj.rearrange("b n p i -> (b n) p i")
        adj_by_row = adj.rearrange("b n p i -> p (b n) i")
        block = ctx.enter_context(nc.Block())

        @block.sync
        def _(sp):
            sp.dma_start(weights_s[:, :], weights_in).then_inc(w_landed, 16)
            for w in range(2):
                cols = slice(w * N // 4, (w + 1) * N // 4)
                sp.dma_start(xt_s[:, cols], xt[:, cols]).then_inc(xt_landed[w], 16)
            for c in range(QUARTERS):
                cols = slice(c * BANK, (c + 1) * BANK)
                sp.dma_start(ring[:, 0, cols], adj[0, 0, :, cols])\
                  .then_inc(first_landed[c - 1] if c else adj_landed[0], 16)
            for k in range(1, RING):
                sp.dma_start(ring[:, k, :], adj[0, k]).then_inc(adj_landed[k], 16)
            sp.dma_start(xn_s[:, block_cols(0)], xn[:, block_cols(0)]).then_inc(xn_landed[0], 16)
            with sp.Fori(1, LAST_FROM // RING) as turn:
                for k in range(RING):
                    sp.wait_ge(mask_ready, through((turn - 1) * RING + k))
                    sp.dma_start(ring[:, k, :], adj_all[turn * RING + k]).then_inc(adj_landed[k], 16)
            for n in range(LAST_FROM // RING * RING, LAST_FROM):
                sp.wait_ge(mask_ready, through(n - RING))
                sp.dma_start(ring[:, n % RING, :], adj_all[n]).then_inc(adj_landed[n % RING], 16)
            for n, load, piece in last_pieces():
                sp.wait_ge(mask_ready, through(n - RING))
                sp.dma_start(piece_of(ring, n % RING, piece), piece_of(adj_by_row, load, piece))\
                  .then_inc(adj_landed[n % RING], 16)

            sp.dma_start(xn_s[:, block_cols(1)], xn[:, block_cols(1)]).then_inc(xn_landed[1], 16)
            for b in range(BLOCKS):
                for p in range(PARTS):
                    sp.wait_ge(y_ready[p], b + 1)
                    sp.dma_start(out[:, x_cols(b, p)], flat(cent_s, p)).then_inc(y_stored[p], 16)
            for p in range(PARTS):
                sp.wait_ge(y_stored[p], 16 * BLOCKS)

        @block.gpsimd
        def _(pool):
            pool.memset(ones[:, :], 1.0).then_inc(ones_ready, 1)
            pool.memset(half_ones[:, :, :], 0.0).then_inc(consts_ready, 1)
            pool.memset(minus_half[:, :], -0.5).then_inc(consts_ready, 1)
            pool.memset(eps_s[:, :], EPS).then_inc(consts_ready, 1)
            pool.wait_ge(consts_ready, 3)
            pool.memset(half_ones[0:D, 0, :], 1.0).then_inc(consts_ready, 1)
            pool.wait_ge(consts_ready, 4)
            pool.memset(half_ones[D:P, 1, :], 1.0).then_inc(consts_ready, 1)
            pool.wait_ge(consts_ready, CONSTS)
            pool.wait_ge(ones_ready, 1)
            pool.affine_select(out=heads[:, :], in_=ones[:, 0:QUARTERS], compare_op=ALU.is_equal, fill=0.0, base=0,
                               pattern=[[-SQUARE, QUARTERS]], channel_multiplier=1).then_inc(heads_ready, 1)
            for half, tiles in enumerate((slice(OWN, JH), slice(JH, JT))):
                pool.wait_ge(v_den_ready, half + 1)
                pool.wait_ge(wh_turned, 2 * half + 2)
                pool.tensor_tensor(v[:, tiles, 0:D], v[:, tiles, 0:D],
                                   v[:, tiles, D:D + 1].to_broadcast([P, tiles.stop - tiles.start, D]),
                                   ALU.mult).then_inc(v_rest_ready, 1)

            def extend_x(b, p):
                if b:
                    pool.wait_ge(dve_epi[p], (b - 1) * DVE_STEPS + X_H)
                pool.wait_ge(dve_epi[p], b * DVE_STEPS + ISO)
                pool.tensor_tensor(xe_s[p][:, :, :],
                                   edgeless_elu[:, :].unsqueeze(1).to_broadcast([P, PART_TILES[p], D]),
                                   over_cols(iso[p][:, :]), ALU.mult).then_inc(pool_epi[p], 1)
                pool.wait_ge(pool_epi[p], b * POOL_STEPS + ISO_ELU)
                pool.tensor_tensor(flat(xe_s, p), flat(xe_s, p), xn_s[:, x_cols(b, p)], ALU.add)\
                    .then_inc(pool_epi[p], 1)

            def centre_rows(b, p):
                pool.wait_ge(dve_epi[p], b * DVE_STEPS + MEAN)
                pool.wait_ge(y_stored[p], 16 * b)
                pool.tensor_tensor(cent_s[p][:, :, :], res_s[p][:, :, :], over_cols(mean[p][:, :]), ALU.subtract)\
                    .then_inc(centred[p], 1)

            def invert_deviation(b, p):
                pool.wait_ge(dve_epi[p], b * DVE_STEPS + VAR)
                pool.tensor_tensor(rstd[p][:, :], var[p][:, :], minus_half[:, 0:PART_TILES[p]], ALU.pow)\
                    .then_inc(pool_epi[p], 1)

            def scale_rows(b, p):
                pool.wait_ge(pool_epi[p], b * POOL_STEPS + RSTD)
                pool.tensor_tensor(cent_s[p][:, :, :], cent_s[p][:, :, :], over_cols(rstd[p][:, :]), ALU.mult)\
                    .then_inc(y_ready[p], 1)

            pool.wait_ge(edgeless_steps, 2)
            pool.wait_ge(xn_landed[0], 16)
            for p in range(PARTS):
                extend_x(0, p)
            for p in range(PARTS):
                invert_deviation(0, p)
                scale_rows(0, p)
            pool.wait_ge(xn_landed[1], 16)
            extend_x(1, 0)
            centre_rows(1, 0)
            for p in PIECES[1]:
                extend_x(1, p)
            invert_deviation(1, 0)
            scale_rows(1, 0)

        @block.scalar
        def _(act):
            def make_mask(n, slot, landed, slot_used):
                act.wait_ge(adj_landed[slot], 16 * landed)
                if slot_used:
                    act.wait_ge(probs_ready, through(n - MASKS))
                act.activation(mask[:, slot % MASKS, :], ring[:, slot, :], ACT.Relu).then_inc(mask_ready, 1)

            def make_first_mask(c):
                act.wait_ge(first_landed[c - 1] if c else adj_landed[0], 16)
                cols = slice(c * BANK, (c + 1) * BANK)
                act.activation(mask[:, 0, cols], ring[:, 0, cols], ACT.Relu).then_inc(mask_ready, 1)

            def make_piece_mask(n, piece):
                act.wait_ge(adj_landed[n % RING], 16 * (n // RING + 1))
                act.wait_ge(probs_ready, through(n - MASKS))
                act.activation(piece_of(mask, n % MASKS, piece), piece_of(ring, n % RING, piece), ACT.Relu)\
                   .then_inc(mask_ready, 1)

            def exp_h(b, p):
                act.wait_ge(dve_epi[p], b * DVE_STEPS + H)
                act.activation(flat(exp_s, p), flat(h_s, p), ACT.Exp).then_inc(h_exp_ready[p], 1)

            def square(b, p):
                act.wait_ge(centred[p], b + 1)
                act.activation(flat(sq_s, p), flat(cent_s, p), ACT.Square).then_inc(sq_ready[p], 1)

            def r_chunk(c):
                act.wait_ge(f_ready, c + 1)
                act.activation(r[:, c * BANK:(c + 1) * BANK], ps[:, F_BANKS[c], :], ACT.Exp,
                               bias=bias_q[:, :], scale=-(1 - SLOPE)).then_inc(r_exp, 1)

            def exp_q(half):
                tiles = slice(half * JH, (half + 1) * JH)
                act.wait_ge(gt_ready, half + 1)
                act.activation(q[:, tiles], gt[:, tiles, 0], ACT.Exp, bias=bias_q[:, :], scale=1 - SLOPE)\
                   .then_inc(q_ready, 1)

            def exp_f(half):
                tiles = slice(half * JH, (half + 1) * JH)
                act.activation(v[:, tiles, D:V], gt[:, tiles, :], ACT.Exp, bias=bias_f[:, :], scale=SLOPE)\
                   .then_inc(v_den_ready, 1)

            for c in range(QUARTERS - 1):
                make_first_mask(c)
            act.wait_ge(biases_ready, 2)
            exp_q(0)
            r_chunk(0)
            exp_f(0)
            for c in range(1, FC // 2):
                r_chunk(c)
            make_first_mask(QUARTERS - 1)
            for k in range(1, HEAD):
                make_mask(k, k % RING, k // RING + 1, k >= MASKS)
                if k == 2:
                    exp_q(1)
                    exp_f(1)
                if k == 3:
                    act.wait_ge(xt_landed[0], 16)
                    act.wait_ge(xt_landed[1], 16)
                    act.activation(r[:, N // 2:N], xt_s[:, :], ACT.Copy, accum_out=x_sum[:, :])\
                       .then_inc(x_sum_ready, 1)
                if k in R_AT:
                    act.wait_ge(x_sum_ready, 1)
                    r_chunk(FC // 2 + R_AT.index(k))
            with act.Fori(HEAD // RING, LOADS // RING) as turn:
                for k in range(RING):
                    make_mask(turn * RING + k, k, turn + 1, True)
            act.wait_ge(mean_wh_ready, 2)
            act.activation(exp_wh[:, :], exp_wh[:, :], ACT.Exp).then_inc(exp_wh_ready, 1)
            for k in range(LOADS - LAST):
                n = LOADS + k
                make_mask(n, n % RING, n // RING + 1, True)
                for p in range(PARTS):
                    if k == EXP_AT[p]:
                        exp_h(0, p)
                    if k == SQ_AT[p]:
                        square(0, p)
            for n, load, piece in last_pieces():
                make_piece_mask(n, piece)
            exp_h(1, 0)
            square(1, 0)
            for p in PIECES[1]:
                exp_h(1, p)
            act.wait_ge(ones_ready, 1)
            act.wait_ge(consts_ready, CONSTS)
            act.activation(sqrt_unread[:, :], ones[:, 0:1], ACT.Sqrt).then_inc(sqrt_loaded, 1)
            for p in PIECES[1]:
                square(1, p)
            for p in PIECES[1]:
                act.wait_ge(dve_epi[p], DVE_STEPS + SQ_SUM)
                act.activation(dev[p][:, :], sq_sum[p][:, :], ACT.Sqrt, bias=eps_s[:, :], scale=1.0 / D)\
                   .then_inc(dev_ready[p], 1)

        @block.vector
        def _(dve):
            r_blocks = r[:, :].rearrange("p (b i) -> p b i", i=BLOCK)

            def weights(b, n, slot, jt, slot_used):
                dve.wait_ge(mask_ready, through(n))
                if slot_used:
                    dve.wait_ge(probs_used, n - PROBS + 1)
                dve.scalar_tensor_tensor(out=probs[:, slot % PROBS, :], in0=r[:, b * BLOCK:(b + 1) * BLOCK],
                                         scalar=q[:, bass.ds(jt, 1)], in1=mask[:, slot % MASKS, :],
                                         op0=ALU.max, op1=ALU.min).then_inc(probs_ready, 1)

            def first_weights(c):
                dve.wait_ge(mask_ready, c + 1)
                dve.wait_ge(r_ready, c + 1)
                cols = slice(c * BANK, (c + 1) * BANK)
                dve.scalar_tensor_tensor(out=probs[:, 0, cols], in0=r[:, cols], scalar=q[:, 0:1],
                                         in1=mask[:, 0, cols], op0=ALU.max, op1=ALU.min).then_inc(probs_ready, 1)

            def piece_weights(n, load, piece):
                dve.wait_ge(mask_ready, through(n))
                dve.wait_ge(probs_used, n - PROBS + 1)
                dve.scalar_tensor_tensor(out=piece_of(probs, n % PROBS, piece),
                                         in0=piece_of(r_blocks, BLOCKS - 1, piece),
                                         scalar=q[:, load - LOADS:load - LOADS + 1],
                                         in1=piece_of(mask, n % MASKS, piece),
                                         op0=ALU.max, op1=ALU.min).then_inc(probs_ready, 1)

            def squares(b, parts, sums):
                return ps[:, SETS[b][sums], cols_of(parts)].rearrange("p (t s) -> p t s", s=SQUARE)

            def early_tiles(p):
                at = sum(PART_TILES[PIECES[1][0]:p])
                return slice(at, at + PART_TILES[p])

            def turn_early():
                dve.wait_ge(probs_used, TOTAL)
                dve.transpose(early_den[:, :, :], squares(BLOCKS - 1, PIECES[1], 2)).then_inc(early_turned, 1)
                dve.transpose(early_h[:, :, 0:SQUARE], squares(BLOCKS - 1, PIECES[1], 0)).then_inc(early_turned, 1)
                dve.transpose(early_h[:, :, SQUARE:D], squares(BLOCKS - 1, PIECES[1], 1)).then_inc(early_turned, 1)

            def turn_sums(b, p):
                late = is_late(b, p)
                at = 0 if late else b
                dve.wait_ge(probs_used, TOTAL + LAST if late else (b + 1) * LOADS)
                dve.transpose(den_s[p][:, :, :], squares(at, (p,), 2)).then_inc(dve_epi[p], 1)
                dve.transpose(h_s[p][:, :, 0:SQUARE], squares(at, (p,), 0)).then_inc(dve_epi[p], 1)
                if late:
                    dve.wait_ge(dve_epi[p], b * DVE_STEPS + TURN_DEN)
                    dve.wait_ge(early_turned, 3)
                    dve.tensor_tensor(den_s[p][:, :, 0], den_s[p][:, :, 0], early_den[:, early_tiles(p), 0], ALU.add)\
                       .then_inc(late_added[p], 1)
                dve.transpose(h_s[p][:, :, SQUARE:D], squares(at, (p,), 1)).then_inc(dve_epi[p], 1)
                if late:
                    dve.wait_ge(late_added[p], 1)
                dve.wait_ge(dve_epi[p], b * DVE_STEPS + TURN_DEN)
                dve.tensor_scalar(iso[p][:, :], den_s[p][:, :, 0], 0.0, None, ALU.is_equal).then_inc(dve_epi[p], 1)
                dve.scalar_tensor_tensor(out=den[p][:, :], in0=den_s[p][:, :, 0], scalar=0.0, in1=den_s[p][:, :, 0],
                                         op0=ALU.is_equal, op1=ALU.add).then_inc(dve_epi[p], 1)

            def divide(b, p):
                past = b * DVE_STEPS
                late = is_late(b, p)
                dve.wait_ge(dve_epi[p], past + TURN_HIGH)
                if late:
                    dve.tensor_tensor(h_s[p][:, :, :], h_s[p][:, :, :], early_h[:, early_tiles(p), :], ALU.add)\
                       .then_inc(late_added[p], 1)
                dve.wait_ge(dve_epi[p], past + DEN)
                dve.reciprocal(rden[p][:, :], den[p][:, :]).then_inc(dve_epi[p], 1)
                dve.wait_ge(dve_epi[p], past + RDEN)
                if late:
                    dve.wait_ge(late_added[p], 2)
                dve.tensor_tensor(h_s[p][:, :, :], h_s[p][:, :, :], over_cols(rden[p][:, :]), ALU.mult)\
                   .then_inc(dve_epi[p], 1)

            def add_h(b, p):
                dve.wait_ge(dve_epi[p], b * DVE_STEPS + H)
                dve.wait_ge(pool_epi[p], b * POOL_STEPS + XE)
                dve.scalar_tensor_tensor(out=flat(res_s, p), in0=flat(h_s, p), scalar=0.0, in1=flat(xe_s, p),
                                         op0=ALU.max, op1=ALU.add).then_inc(dve_epi[p], 1)

            def add_exp(b, p):
                dve.wait_ge(dve_epi[p], b * DVE_STEPS + X_H)
                dve.wait_ge(h_exp_ready[p], b + 1)
                dve.scalar_tensor_tensor(out=flat(res_s, p), in0=flat(exp_s, p), scalar=1.0, in1=flat(res_s, p),
                                         op0=ALU.min, op1=ALU.add).then_inc(dve_epi[p], 1)

            def average(b, p):
                dve.wait_ge(dve_epi[p], b * DVE_STEPS + RES)
                dve.reduce_sum(row_sum[p][:, :], res_s[p][:, :, :], AX_X).then_inc(dve_epi[p], 1)
                dve.wait_ge(dve_epi[p], b * DVE_STEPS + ROW_SUM)
                dve.tensor_scalar(mean[p][:, :], row_sum[p][:, :], 1.0 / D, None, ALU.mult)\
                   .then_inc(dve_epi[p], 1)

            def centre(b, p):
                dve.wait_ge(dve_epi[p], b * DVE_STEPS + MEAN)
                if b:
                    dve.wait_ge(y_stored[p], 16 * b)
                dve.tensor_tensor(cent_s[p][:, :, :], res_s[p][:, :, :], over_cols(mean[p][:, :]), ALU.subtract)\
                   .then_inc(centred[p], 1)

            def sum_squares(b, p):
                dve.wait_ge(sq_ready[p], b + 1)
                dve.reduce_sum(sq_sum[p][:, :], sq_s[p][:, :, :], AX_X).then_inc(dve_epi[p], 1)
                if not is_late(b, p):
                    dve.wait_ge(dve_epi[p], b * DVE_STEPS + SQ_SUM)
                    dve.tensor_scalar(var[p][:, :], sq_sum[p][:, :], 1.0 / D, EPS, ALU.mult, ALU.add)\
                       .then_inc(dve_epi[p], 1)

            def invert(p):
                dve.wait_ge(dev_ready[p], 1)
                dve.reciprocal(rstd[p][:, :], dev[p][:, :]).then_inc(rstd_ready[p], 1)

            def scale_rows(b, p):
                dve.wait_ge(rstd_ready[p], 1)
                dve.tensor_tensor(cent_s[p][:, :, :], cent_s[p][:, :, :], over_cols(rstd[p][:, :]), ALU.mult)\
                   .then_inc(y_ready[p], 1)

            def cap_r(c):
                dve.wait_ge(r_exp, c + 1)
                cols = slice(c * BANK, (c + 1) * BANK)
                dve.tensor_scalar(r[:, cols], r[:, cols], 1.0, None, ALU.min).then_inc(r_ready, 1)

            def turn_wh(half, part):
                dve.wait_ge(wh_ready, 2 * half + part + 1)
                dve.transpose(v[:, half * JH:(half + 1) * JH, part * SQUARE:(part + 1) * SQUARE],
                              ps[:, WH_BANKS[part], :].rearrange("p (t s) -> p t s", s=SQUARE))\
                   .then_inc(wh_turned, 1)

            def find_edge(half):
                dve.wait_ge(g_ready, half + 1)
                dve.reduce_max(g_edge[:, half:half + 1], ps[:, SPARE[half], :], AX_X).then_inc(edge_ready, 1)
                dve.wait_ge(edge_ready, half + 1)
                dve.tensor_scalar(g_heads[:, half, :], heads[:, :], g_edge[:, half:half + 1], None, ALU.mult)\
                   .then_inc(g_heads_ready, 1)

            def turn_g(half):
                dve.transpose(gt[:, half * JH:(half + 1) * JH, :],
                              ps[:, SPARE[half], :].rearrange("p (t s) -> p t s", s=SQUARE)).then_inc(gt_ready, 1)

            dve.wait_ge(wa_ready, 1)
            dve.wait_ge(consts_ready, CONSTS)
            dve.tensor_scalar(wa2[:, :, :], half_ones[:, :, 0:SQUARE], ps[:, SMALL, 1:2], None, ALU.mult)\
               .then_inc(wa2_ready, 1)
            dve.tensor_scalar(wa1[:, :, :], half_ones[:, :, :], ps[:, SMALL, 0:1], None, ALU.mult)\
               .then_inc(wa1_ready, 1)
            dve.wait_ge(heads_ready, 1)
            dve.wait_ge(ones_ready, 1)
            find_edge(0)
            turn_g(0)
            turn_wh(0, 0)
            find_edge(1)
            dve.wait_ge(g_heads_spread, 1)
            dve.reduce_max(g_max[:, :], ps[:, SMALL, 0:2 * QUARTERS], AX_X).then_inc(g_max_ready, 1)
            dve.wait_ge(g_max_ready, 1)
            dve.tensor_scalar(bias_q[:, :], g_max[:, :], -(1 - SLOPE), None, ALU.mult).then_inc(biases_ready, 1)
            dve.tensor_scalar(bias_f[:, :], g_max[:, :], -SLOPE, None, ALU.mult).then_inc(biases_ready, 1)
            turn_wh(0, 1)
            cap_r(0)
            dve.wait_ge(v_den_ready, 1)
            dve.wait_ge(wh_turned, 2)
            dve.tensor_tensor(v[:, 0:OWN, 0:D], v[:, 0:OWN, 0:D], v[:, 0:OWN, D:D + 1].to_broadcast([P, OWN, D]),
                              ALU.mult).then_inc(v_ready, 1)
            dve.wait_ge(q_ready, 1)
            for c in range(QUARTERS):
                if c < QUARTERS - 1:
                    cap_r(c + 1)
                first_weights(c)
            for k in range(1, HEAD):
                weights(0, k, k, k, k >= PROBS)
                if k == 1:
                    turn_g(1)
                if k == 2:
                    turn_wh(1, 0)
                if k == 3:
                    turn_wh(1, 1)
                if k == 4:
                    dve.wait_ge(x_sum_ready, 1)
                    dve.tensor_scalar(x_sums[:, :], ones[:, :], x_sum[:, 0:1], None, ALU.mult)\
                       .then_inc(x_sums_ready, 1)
                if k in CAP_AT:
                    cap_r(FC // 2 + CAP_AT.index(k))
            dve.wait_ge(q_ready, 2)
            with dve.Fori(HEAD // RING, LOADS // RING) as turn:
                for k in range(RING):
                    weights(0, turn * RING + k, k, turn * RING + k, True)
            dve.wait_ge(sum_wh_summed, 1)
            dve.tensor_scalar(mean_wh[:, :], ps[:, SPARE[0], 0:D], 1.0 / N, None, ALU.mult)\
               .then_inc(mean_wh_ready, 1)
            dve.tensor_scalar(exp_wh[:, :], ps[:, SPARE[0], 0:D], 1.0 / N, 0.0, ALU.mult, ALU.min)\
               .then_inc(mean_wh_ready, 1)
            dve.wait_ge(r_ready, FC)
            steps = (turn_sums, divide, add_h, add_exp, average, centre, sum_squares)
            for k in range(LOADS - LAST):
                n = LOADS + k
                weights(1, n, n % RING, k, True)
                if k == 1:
                    dve.wait_ge(exp_wh_ready, 1)
                    dve.tensor_scalar(exp_wh[:, :], exp_wh[:, :], -1.0, None, ALU.add)\
                       .then_inc(edgeless_steps, 1)
                    dve.wait_ge(edgeless_steps, 1)
                    dve.wait_ge(mean_wh_ready, 2)
                    dve.scalar_tensor_tensor(out=edgeless_elu[:, :], in0=mean_wh[:, :], scalar=0.0,
                                             in1=exp_wh[:, :], op0=ALU.max, op1=ALU.add)\
                       .then_inc(edgeless_steps, 1)
                for p in range(PARTS):
                    if k in EPILOGUE_AT[p]:
                        steps[EPILOGUE_AT[p].index(k)](0, p)
            pieces = last_pieces()
            for numbers in pieces[:LAST + AHEAD]:
                piece_weights(*numbers)
            turn_sums(1, 0)
            for numbers in pieces[LAST + AHEAD:]:
                piece_weights(*numbers)
            divide(1, 0)
            turn_early()
            add_h(1, 0)
            add_exp(1, 0)
            average(1, 0)
            for p in PIECES[1]:
                turn_sums(1, p)
            for p in PIECES[1]:
                divide(1, p)
            sum_squares(1, 0)
            for step in (add_h, add_exp, average, centre, sum_squares):
                for p in PIECES[1]:
                    step(1, p)
            for p in PIECES[1]:
                invert(p)
                scale_rows(1, p)

        @block.tensor
        def _(pe):
            def quarter(c):
                return slice(c * SQUARE, (c + 1) * SQUARE)

            def warm(products):
                for _ in range(products):
                    pe.matmul(ps[:, 0, 0:P], ones[:, :], ones[:, :], start=True, stop=True)

            def make_g(half):
                pe.wait_ge(xt_landed[half], 16)
                for b in range(2):
                    for c in range(2):
                        at = (half * 2 + c) * BANK
                        mm = pe.matmul(ps[quarter(b * 2 + c), SPARE[half], :], wa2[:, b, :], xt_s[:, at:at + BANK],
                                       start=True, stop=True)
                mm.then_inc(g_ready, 1)

            def make_wh(half, part):
                for b in range(2):
                    for c in range(2):
                        at = (half * 2 + c) * BANK
                        mm = pe.matmul(ps[quarter(b * 2 + c), WH_BANKS[part], :], w_s[b][:, quarter(part)],
                                       xt_s[:, at:at + BANK], start=True, stop=True)
                mm.then_inc(wh_ready, 1)

            def make_f(c):
                half, at = c // (FC // 2), c % (FC // 2) * BANK
                pe.matmul(ps[:, F_BANKS[c], :], wa1[:, half, :], xt_s[:, at:at + BANK],
                          start=True, stop=True).then_inc(f_ready, 1)

            pe.wait_ge(ones_ready, 1)
            warm(WARM[0])
            pe.wait_ge(w_landed, 16)
            pe.matmul(ps[:, SMALL, 0:2], wt_s, a_s, start=True, stop=True).then_inc(wa_ready, 1)
            warm(WARM[1])
            pe.wait_ge(wa2_ready, 1)
            make_g(0)
            make_wh(0, 0)
            make_g(1)
            make_wh(0, 1)
            pe.wait_ge(wa1_ready, 1)
            pe.wait_ge(g_heads_ready, 2)
            pe.matmul(ps[:, SMALL, 0:2 * QUARTERS], ones[:, :], g_heads[:, :, :].rearrange("p u c -> p (u c)"),
                      start=True, stop=True).then_inc(g_heads_spread, 1)
            make_f(0)
            make_f(1)
            make_f(2)
            pe.wait_ge(g_max_ready, 1)
            make_f(3)
            pe.wait_ge(wh_turned, 2)
            make_wh(1, 0)
            make_wh(1, 1)
            pe.wait_ge(gt_ready, 1)
            make_f(4)
            pe.wait_ge(r_exp, 4)
            make_f(5)

            def add_load(b, jt):
                n = b * LOADS + jt
                pe.wait_ge(probs_ready, through(n))
                for part in range(V // SQUARE):
                    for c in range(QUARTERS):
                        mm = pe.matmul(ps[quarter(c), SETS[b][part], :], v[:, jt, quarter(part)],
                                       probs[:, n % PROBS, c * BANK:(c + 1) * BANK],
                                       start=(jt == 0), stop=(jt == JT - 1))
                mm.then_inc(probs_used, 1)

            def add_piece(n, load, piece):
                b, jt = load // LOADS, load % LOADS
                weights = piece_of(probs, n % PROBS, piece)
                pe.wait_ge(probs_ready, through(n))
                for part in range(V // SQUARE):
                    for c in range(QUARTERS):
                        mm = pe.matmul(ps[quarter(c), SETS[b - piece][part], cols_of(PIECES[piece])],
                                       v[:, jt, quarter(part)], weights[:, c, :],
                                       start=(piece == 1 and load == LAST_FROM), stop=(load == TOTAL - 1))
                mm.then_inc(probs_used, 1)

            pe.wait_ge(v_ready, 1)
            for jt in range(JT):
                if jt == OWN:
                    pe.wait_ge(v_rest_ready, 1)
                if jt == JH:
                    pe.wait_ge(v_rest_ready, 2)
                add_load(0, jt)
                if jt == F_AT[0]:
                    pe.wait_ge(gt_ready, 2)
                    make_f(6)
                if jt == F_AT[1]:
                    pe.wait_ge(r_exp, 5)
                    make_f(7)
                if jt == SUM_WH_AT:
                    pe.wait_ge(x_sums_ready, 1)
                    pe.wait_ge(r_exp, FC)
                    pe.matmul(ps[:, SPARE[0], 0:D], x_sums[:, :], w_s[0], start=True, stop=False)
                    pe.matmul(ps[:, SPARE[0], 0:D], x_sums[:, :], w_s[1], start=False, stop=True)\
                      .then_inc(sum_wh_summed, 1)
            for jt in range(JT - LAST):
                add_load(1, jt)
            for n, load, piece in last_pieces():
                add_piece(n, load, piece)


def kernel(x, adj, L0_gnn_W, L0_gnn_a):
    import numpy as np
    import concourse.bacc as bacc
    from concourse.bass_utils import run_bass_kernel_spmd

    x, adj, W, a = (np.asarray(t) for t in (x, adj, L0_gnn_W, L0_gnn_a))
    N, D = x.shape
    order = np.arange(N).reshape(BLOCKS, QUARTERS, SQUARE, TILES).transpose(0, 1, 3, 2)
    j_order = order.reshape(BLOCKS, 2, 2, TILES, SQUARE).transpose(1, 3, 0, 2, 4).ravel()
    order = order.ravel()
    adj_rows = np.ascontiguousarray(adj.T)[j_order][:, order]
    arrays = {
        "xt": np.ascontiguousarray(x[order].T.reshape(D, 2, N // 2).transpose(1, 0, 2)).reshape(2 * D, N // 2),
        "xn": np.ascontiguousarray(x.reshape(BLOCKS, P, TILES * D).transpose(1, 0, 2)).reshape(P, N // P * D),
        "weights": np.concatenate([np.pad(W, ((0, D), (0, 0))), np.pad(W, ((D, 0), (0, 0))),
                                   np.tile(W.T, (2, 2)), np.tile(a.reshape(2, D).T, (2, 1))], axis=1),
        "adj": np.ascontiguousarray(adj_rows.reshape(N // P, P, BLOCKS, BLOCK).transpose(2, 0, 1, 3)),
    }
    nc = bacc.Bacc("TRN2", target_bir_lowering=False, num_devices=1)
    ins = {name: nc.dram_tensor(f"in_{name}", t.shape, mybir.dt.from_np(t.dtype), kind="ExternalInput").ap()
           for name, t in arrays.items()}
    out = nc.dram_tensor("out", (P, N // P * D), F32, kind="ExternalOutput").ap()
    gat_layer(nc, ins["xt"], ins["xn"], ins["weights"], ins["adj"], out)
    got = run_bass_kernel_spmd(nc, [{f"in_{name}": t for name, t in arrays.items()}], core_ids=[0])
    y = got.results[0]["out"]
    return y.reshape(P, BLOCKS, TILES, D).transpose(1, 0, 2, 3).reshape(N, D)
```
